# Optimizing a Trainium2 kernel written in Bass

```python
import numpy as np
import jax
import jax.numpy as jnp

def _softmax(x, axis=-1):
    return jax.nn.softmax(x, axis=axis)

def _gelu(x):
    return jax.nn.gelu(x, approximate=True)

def _silu(x):
    return jax.nn.silu(x)

def _sigmoid(x):
    return jax.nn.sigmoid(x)

def _layernorm(x, axis=-1, eps=1e-05):
    m = jnp.mean(x, axis=axis, keepdims=True)
    v = jnp.var(x, axis=axis, keepdims=True)
    return (x - m) / jnp.sqrt(v + eps)

def _scatter_add(tgt, idx, src, axis=0):
    return tgt.at[idx].add(src)

def _segment_sum(src, seg, n):
    return jax.ops.segment_sum(src, seg, n)
kernel_name = 'mk_sandwich_d1_jaxref_r4_1ea75f'

def setup_inputs(seed: int=0):
    np.random.seed(seed)
    _w = jnp.asarray

    def _L0_attn_setup():
        import jax, jax.numpy as jnp
        import numpy as np
        DIM = 1024
        N_HEADS = 32
        HEAD_DIM = DIM // N_HEADS
        key = jax.random.key(seed)
        k0, k1, k2, k3, k4 = jax.random.split(key, 5)
        B, T = (2, 512)
        x = jax.random.normal(k0, (B, T, DIM), dtype=jnp.float32)
        s = 1.0 / np.sqrt(DIM)
        wq = jax.random.normal(k1, (DIM, DIM), dtype=jnp.float32) * s
        wk = jax.random.normal(k2, (DIM, HEAD_DIM), dtype=jnp.float32) * s
        wv = jax.random.normal(k3, (DIM, HEAD_DIM), dtype=jnp.float32) * s
        wo = jax.random.normal(k4, (DIM, DIM), dtype=jnp.float32) * s
        return {'x': x, 'wq': wq, 'wk': wk, 'wv': wv, 'wo': wo}
    _L0_attn_in = _L0_attn_setup()

    def _L0_ffn_setup():
        import jax, jax.numpy as jnp
        import numpy as np
        ALPHA = 32
        R = 16
        SCALING = ALPHA / R
        key = jax.random.key(seed)
        k1, k2, k3, k4 = jax.random.split(key, 4)
        B_, S, D = (4, 512, 1024)
        H, r, O = (8, R, 1024)
        x = jax.random.normal(k1, (B_, S, D), dtype=jnp.float32)
        A = jax.random.normal(k2, (H, r, D), dtype=jnp.float32) * 0.02
        Bm = jax.random.normal(k3, (H, O, r), dtype=jnp.float32) * 0.02
        Wr = jax.random.normal(k4, (H, D), dtype=jnp.float32) * 0.02
        br = jnp.zeros((H,), dtype=jnp.float32)
        return {'x': x, 'A': A, 'B': Bm, 'Wr': Wr, 'br': br}
    _L0_ffn_in = _L0_ffn_setup()
    _d = {'L0_attn_x': _L0_attn_in['x'], 'L0_attn_wq': _L0_attn_in['wq'], 'L0_attn_wk': _L0_attn_in['wk'], 'L0_attn_wv': _L0_attn_in['wv'], 'L0_attn_wo': _L0_attn_in['wo'], 'L0_ffn_A': _L0_ffn_in['A'], 'L0_ffn_B': _L0_ffn_in['B'], 'L0_ffn_Wr': _L0_ffn_in['Wr'], 'L0_ffn_br': _L0_ffn_in['br']}
    _x0 = _d['L0_attn_x']
    _d['L0_attn_x'] = jax.random.normal(jax.random.fold_in(jax.random.key(seed), 1), (2, 2048, 1024), dtype=_x0.dtype)
    del _x0
    return _d

def reference(L0_attn_x, L0_attn_wq, L0_attn_wk, L0_attn_wv, L0_attn_wo, L0_ffn_A, L0_ffn_B, L0_ffn_Wr, L0_ffn_br):

    def _L0_attn_ref(x, wq, wk, wv, wo):
        import jax, jax.numpy as jnp
        import numpy as np
        DIM = 1024
        N_HEADS = 32
        HEAD_DIM = DIM // N_HEADS
        B, T, C = x.shape
        q = (x @ wq).reshape(B, T, N_HEADS, HEAD_DIM)
        k = x @ wk
        v = x @ wv
        scale = 1.0 / jnp.sqrt(jnp.asarray(HEAD_DIM, dtype=x.dtype))
        scores = jnp.einsum('bqhd,bkd->bhqk', q, k) * scale
        causal = jnp.tril(jnp.ones((T, T), dtype=bool))
        scores = jnp.where(causal[None, None], scores, -jnp.inf)
        probs = jax.nn.softmax(scores.astype(jnp.float32), axis=-1).astype(x.dtype)
        out = jnp.einsum('bhqk,bkd->bqhd', probs, v).reshape(B, T, C)
        return out @ wo

    def _L0_ffn_ref(x, A, B, Wr, br):
        import jax, jax.numpy as jnp
        import numpy as np
        ALPHA = 32
        R = 16
        SCALING = ALPHA / R
        H = A.shape[0]
        router_logits = jnp.einsum('bsd,hd->bsh', x, Wr) + br
        scores = H * jax.nn.softmax(router_logits, axis=-1)
        low = jnp.einsum('bsd,hrd->bshr', x, A)
        out = jnp.einsum('bshr,hor,bsh->bso', low, B, scores)
        return SCALING * out
    x = L0_attn_x
    x = x + _layernorm(_L0_attn_ref(_layernorm(x, axis=-1), L0_attn_wq, L0_attn_wk, L0_attn_wv, L0_attn_wo), axis=-1)
    x = x + _layernorm(_L0_ffn_ref(_layernorm(x, axis=-1), L0_ffn_A, L0_ffn_B, L0_ffn_Wr, L0_ffn_br), axis=-1)
    return x

_drawn_inputs = setup_inputs


def setup_inputs(seed=0):
    import zlib

    import numpy as np

    out = dict(_drawn_inputs(seed))
    spreads = {'L0_ffn_br': (0.0, 0.1)}
    factors = {}
    for name, (base, spread) in spreads.items():
        noise = np.random.default_rng([zlib.crc32(name.encode()), seed]).standard_normal(out[name].shape)
        drawn = base * np.exp(spread * noise) if base else spread * noise
        out[name] = jnp.asarray(drawn.astype(out[name].dtype))
    for name, factor in factors.items():
        out[name] = (out[name] * factor).astype(out[name].dtype)
    return out
```

```python
import concourse.bass as bass
from concourse import mybir
from contextlib import ExitStack


def bass_mqa_sandwich_lora_router(nc, x, wq, wk, wv, wo, ffn_a, ffn_b, ffn_wr, ffn_br, out):
    F32, F32R, BF16 = mybir.dt.float32, mybir.dt.float32r, mybir.dt.bfloat16
    ALU, ACT, AX = mybir.AluOpType, mybir.ActivationFunctionType, mybir.AxisListType

    P = 128
    NB, NT, D = x.shape
    HD = wk.shape[1]
    NH = wq.shape[1] // HD
    GH = P // HD
    NU = NH // GH
    KT = D // P
    BLK = 512
    TB = BLK // P
    NQ = NT // BLK
    HALF = 512
    NF, RANK, _ = ffn_a.shape
    HR = NF * RANK
    SCALE = float(HD) ** -0.5
    SCALING = 32.0 / RANK
    EPS = 1e-5
    NEG = -1e30
    STK = 3 * HD
    NP_ = 3

    def steps_of(qb):
        return TB * (qb + 1)

    STEPS = NU * sum(steps_of(q) for q in range(NQ))

    def base_counts(b, qb, r):
        T, blk = steps_of(qb), b * NQ + qb
        step = b * STEPS + NU * sum(steps_of(q) for q in range(qb)) + r * (NP_ * T)
        unit = b * (NQ * NU) + qb * NU + r * NP_
        return dict(
            block=blk, tile=blk * TB, unit=unit,
            step=step, step4=step * GH,
            add=b * (STEPS - NQ * NU) + NU * sum(steps_of(q) - 1 for q in range(qb)) + r * (NP_ * (T - 1)),
            unit_of_first=b * NU + r * NP_,
            wq=blk * (16 * NP_) + r * 16,
            **{f"{name}{n}": blk * (d * n) + r * d
               for name, d in (("stack", 16 * 3 * GH), ("rows", 16 * GH)) for n in set(UNITS_OF_SLOT)})

    UNITS_OF_SLOT = [len(range(i, NU, NP_)) for i in range(NP_)]

    def frame(engine, b, qb, r):
        return dict(b=b, r=r, **{k: engine.snap(v) for k, v in base_counts(b, qb, r).items()})

    def unit0(f, u):
        return f["unit"] + u[1]

    def step0(f, qb, u):
        return f["step"] + u[1] * steps_of(qb)

    def head0(f, qb, u):
        return f["step4"] + GH * u[1] * steps_of(qb)

    def adds0(f, qb, u):
        return f["add"] + u[1] * (steps_of(qb) - 1)

    def filled(f, name, u):
        d = 16 * 3 * GH if name == "stack" else 16 * GH
        return f[f"{name}{UNITS_OF_SLOT[u[1] % NP_]}"] + d * (u[1] // NP_ + 1)

    def lead_of(qb):
        return max(1, steps_of(qb) // 4)

    x_t = x.rearrange("b (n p) d -> (b n) p d", p=P)
    out_t = out.rearrange("b (n p) d -> (b n) p d", p=P)
    wq_v = wq.rearrange("(k p) m -> p k m", p=P)
    wo_v = wo.rearrange("(k p) m -> p k m", p=P)
    wk_v = wk.rearrange("(k p) m -> p k m", p=P)
    wv_v = wv.rearrange("(k p) m -> p k m", p=P)
    fb_v = ffn_b.rearrange("h (n p) r -> n p h r", p=P)

    ctx = ExitStack()
    with ctx:
        def sb(name, shape, dt=F32):
            return ctx.enter_context(nc.sbuf_tensor(name, shape, dt))

        def sem(name):
            return ctx.enter_context(nc.semaphore(name))

        wo_sb = sb("wo_sb", [P, KT, D])
        wkv_sb = sb("wkv_sb", [P, KT, 4 * HD])
        wq_sb = sb("wq_sb", [P, 3, KT, P])
        fa_sb = sb("fa_sb", [P, KT, HR + NF])
        fb_sb = sb("fb_sb", [HR, D])
        br_sb = sb("br_sb", [P, NF])
        ident = sb("ident", [P, P])
        identb = sb("identb", [P, P], BF16)
        mask_qk = sb("mask_qk", [P, P], BF16)
        mask_kq = sb("mask_kq", [P, P], BF16)
        ones = sb("ones", [P, HD])
        eps_sb = sb("eps_sb", [P, 1])
        xs = sb("xs", [P, TB, D])
        xn = sb("xn", [P, 2, D])
        zs = sb("zs", [P, 2, D])
        xT = sb("xT", [P, KT, BLK])
        ks = sb("ks", [P, NT], F32R)
        k1t = sb("k1t", [P, BLK], F32R)
        vT = sb("vT", [P, BLK])
        vs = sb("vs", [P, NT // P, HD])
        q1 = sb("q1", [P, BLK], F32R)
        q2 = sb("q2", [P, BLK], F32R)
        qs = sb("qs", [P, NP_, GH, BLK], F32R)
        mx = sb("mx", [P, TB * GH, NQ])
        negm = sb("negm", [P, TB * GH])
        mz = sb("mz", [P, TB, GH, 2])
        mT = sb("mT", [2 * GH, BLK], F32R)
        pr = sb("pr", [P, NP_, GH, BLK])
        ds = sb("ds", [P, GH, BLK])
        rden = sb("rden", [P, BLK])
        ao = sb("ao", [P, NU, BLK])
        scratch = sb("scratch", [P, 4])
        lg = sb("lg", [P, 2, NF])
        nlm = sb("nlm", [P, 2, 1])
        le = sb("le", [P, 2, NF])
        ls = sb("ls", [P, 2, 1])
        lr = sb("lr", [P, 2, 1])
        lw = sb("lw", [P, 2, NF])
        sl = sb("sl", [P, 2, HR])
        slT = sb("slT", [P, 2, P])
        LN = {}
        for kind, n in (("pre", TB), ("att", 1), ("mid", 1), ("ffn", 1)):
            LN[kind] = dict(
                n=n, st=sb(f"st_{kind}", [P, n, 2, 6]), mv=sb(f"mv_{kind}", [P, n, 2]),
                ln=sb(f"ln_{kind}", [P, n]), ex=sb(f"ex_{kind}", [P, n]), ve=sb(f"ve_{kind}", [P, n]),
                t1=sb(f"t1_{kind}", [P, n]), t2=sb(f"t2_{kind}", [P, n]), t3=sb(f"t3_{kind}", [P, n]),
                r=sb(f"r_{kind}", [P, n]), nb=sb(f"nb_{kind}", [P, n]),
                s_st=sem(f"{kind}_stats"), s_mv=sem(f"{kind}_meanvar"), s_ln=sem(f"{kind}_log"),
                s_ex=sem(f"{kind}_rough"), s_ch=sem(f"{kind}_newton"))
        CH = 6

        ps = ctx.enter_context(nc.psum_tensor("ps", [P, 8, HALF], F32))
        PM, PST, PPV, PQ, PAUX = 0, 2, 5, 6, 7

        const_loaded = sem("const_loaded")
        pool_const = sem("pool_const")
        wt_ready = sem("wt_ready")
        wt_read = sem("wt_read")
        x_loaded = [sem(f"x_loaded{i}") for i in range(TB)]
        wq_loaded = [sem(f"wq_loaded{i}") for i in range(3)]
        xn_ready = sem("xn_ready")
        xt_ready = sem("xt_ready")
        xt_act = sem("xt_act")
        xt_dve = sem("xt_dve")
        kv_ready = sem("kv_ready")
        k_act = sem("k_act")
        k_dve = sem("k_dve")
        v_tr = sem("v_tr")
        v_sb = sem("v_sb")
        q_ready = sem("q_ready")
        q1_sb = sem("q1_sb")
        q2_sb = sem("q2_sb")
        qs_loaded = [sem(f"qs_loaded{i}") for i in range(NP_)]
        mx_ready = sem("mx_ready")
        mx_done = sem("mx_done")
        negm_ready = sem("negm_ready")
        mz1_ready = sem("mz1_ready")
        mz_ready = sem("mz_ready")
        mt_ready = sem("mt_ready")
        mt_sb = sem("mt_sb")
        qm_loaded = [sem(f"qm_loaded{i}") for i in range(NP_)]
        st_ready = sem("st_ready")
        exp_done = sem("exp_done")
        pv_done = sem("pv_done")
        pv_sb = sem("pv_sb")
        add_pool = sem("add_pool")
        add_dve = sem("add_dve")
        cp_pool = sem("cp_pool")
        cp_dve = sem("cp_dve")
        den_ready = sem("den_ready")
        rden_ready = sem("rden_ready")
        ao_ready = sem("ao_ready")
        y1_ready = sem("y1_ready")
        z1_ready = sem("z1_ready")
        x1_ready = sem("x1_ready")
        h_ready = sem("h_ready")
        ht_ready = sem("ht_ready")
        ht_act = sem("ht_act")
        ht_dve = sem("ht_dve")
        low_ready = sem("low_ready")
        sm_ch = sem("sm_ch")
        le_ready = sem("le_ready")
        sl_ready = sem("sl_ready")
        slt_ready = sem("slt_ready")
        slt_sb = sem("slt_sb")
        y2_ready = sem("y2_ready")
        z2_ready = sem("z2_ready")
        x2_ready = sem("x2_ready")
        stored = sem("stored")
        passed = sem("passed")

        nc.disable_value_cache = True
        block = ctx.enter_context(nc.Block())

        CREDIT = 3
        AHEAD = 2

        def at(u):
            return u[0] * NP_ + u[1]

        def after(u, n):
            return (u[0], u[1] + n)

        def cols(qb, t):
            return (t - TB * qb) * P if t >= TB * qb else 0, t >= TB * qb

        def item(qb, s):
            c, qt = s // TB, s % TB
            return c, qt, (qt + 1) * P if c == qb else BLK, c == qb

        def normal(qb, u, t):
            return (u, t) if t < steps_of(qb) else (after(u, 1), t - steps_of(qb))

        def schedule(qb, u):
            T, n = steps_of(qb), u[1] if isinstance(u[0], int) else None
            last = n == NU - 1
            return [(u, t) for t in range(AHEAD, T)] + ([] if last else [(after(u, 1), t) for t in range(AHEAD)])

        def static_unit(u):
            return u[1] if isinstance(u[0], int) else None

        def units_left(u, n):
            j = static_unit(u)
            return j is None or j + n < NU

        def blocks(engine, b, prologue, turn):
            for qb in range(NQ):
                f = frame(engine, b, qb, 0)
                prologue(f, qb)
                with engine.Fori(0, (NU - 2) // NP_) as r:
                    g = frame(engine, b, qb, r)
                    for k in range(NP_):
                        turn(g, qb, (r, k))
                f = frame(engine, b, qb, 0)
                turn(f, qb, (0, NU - 2))
                turn(f, qb, (0, NU - 1))
                yield f, qb

        def q_steps(qb):
            n = max(1, steps_of(qb) // 2 - 3)
            per = -(-KT // n)
            return {AHEAD + i: range(i * per, min(KT, (i + 1) * per)) for i in range(n) if i * per < KT}

        POST = [(1, 0), (2, 0), (1, 1), (3, 0), (2, 1), (1, 2), (3, 1), (2, 2), (1, 3), (3, 2), (2, 3), (3, 3)]
        POST_PE = [(1, 0), (1, 1), (2, 0), (1, 2), (3, 0), (2, 1), (1, 3), (3, 1), (2, 2), (3, 2), (2, 3), (3, 3)]


        def wait_apart(engine, s, value):
            engine.wait_ge(s, value)
            engine.sem_inc(passed, 1)

        def sums(engine, ops, added, copied, g0, g1, f, qb, u, t):
            T = steps_of(qb)
            c0, _ = cols(qb, t)
            engine.wait_ge(exp_done, CREDIT + head0(f, qb, u) + GH * t + g1)
            this = pr[:, (u[1] * T + t) % NP_, g0:g1, c0:]
            if t == 1:
                wait_apart(engine, den_ready, 1 + unit0(f, u))
                first = pr[:, (u[1] * T) % NP_, g0:g1, :]
                if c0:
                    ops.tensor_copy(ds[:, g0:g1, 0:c0], first[:, :, 0:c0]).then_inc(copied, 1)
                    engine.wait_ge(copied, f["unit_of_first"] + u[1] + 1)
                ops.tensor_tensor(ds[:, g0:g1, c0:], first[:, :, c0:], this, ALU.add).then_inc(added, 1)
            else:
                engine.wait_ge(added, CREDIT + adds0(f, qb, u) + t - 1)
                ops.tensor_tensor(ds[:, g0:g1, c0:], ds[:, g0:g1, c0:], this, ALU.add).then_inc(added, 1)

        WT = 3 * KT
        POOL_CONST = 10
        SM = 5

        N_CONST = 3 + 1 + 1 + 1 + 1 + 1 + D // P

        @block.sync
        def _(sp):
            for c in range(3):
                sp.dma_start(wkv_sb[:, :, c * HD:(c + 1) * HD], wk_v).then_inc(const_loaded, 16)
            sp.dma_start(wkv_sb[:, :, 3 * HD:4 * HD], wv_v).then_inc(const_loaded, 16)
            sp.dma_start(wo_sb[:, :, :], wo_v).then_inc(const_loaded, 16)
            sp.dma_start(xs[:, 0, :], ffn_a.rearrange("h r d -> (h r) d")).then_inc(const_loaded, 16)
            sp.dma_start(xs[0:NF, 1, :], ffn_wr).then_inc(const_loaded, 16)
            sp.dma_start(br_sb[:, :], ffn_br.partition_broadcast(P)).then_inc(const_loaded, 16)
            for n in range(D // P):
                sp.dma_start(xs[:, 2, n * P:(n + 1) * P].rearrange("p (h r) -> p h r", h=NF),
                             fb_v[n]).then_inc(const_loaded, 16)
            sp.wait_ge(wt_read, WT)

            def load_wq(j, slot):
                sp.dma_start(wq_sb[:, slot, :, :], wq_v[:, :, bass.ds(j * P, P)]).then_inc(wq_loaded[slot], 16)

            def stack(f, qb, u):
                n = unit0(f, u) + 1
                sp.wait_ge(q1_sb, n)
                sp.wait_ge(q2_sb, n)
                slot = u[1] % NP_
                for g in range(GH):
                    for row, part in ((0, q1), (HD, q1), (2 * HD, q2)):
                        sp.dma_start(qs[row:row + HD, slot, g, :].bitcast(F32),
                                     part[g * HD:(g + 1) * HD, :].bitcast(F32)).then_inc(qs_loaded[slot], 16)

            def maxima(f, qb, u):
                sp.wait_ge(mt_sb, unit0(f, u) + 1)
                slot = u[1] % NP_
                for g in range(GH):
                    sp.dma_start(qs[STK:STK + 2, slot, g, :].bitcast(F32),
                                 mT[2 * g:2 * g + 2, :].bitcast(F32)).then_inc(qm_loaded[slot], 16)

            def prologue(f, qb):
                for i in range(TB):
                    sp.dma_start(xs[:, i, :], x_t[f["tile"] + i]).then_inc(x_loaded[i], 16)
                for j in range(3):
                    load_wq(j, j)
                stack(f, qb, (0, 0))
                stack(f, qb, (0, 1))
                maxima(f, qb, (0, 0))

            def turn(f, qb, u):
                r, k = u
                if units_left(u, 2):
                    sp.wait_ge(q_ready, unit0(f, u) + 1)
                    load_wq(5 + 2 * r if k == 2 else at(u) + 3, k)
                    stack(f, qb, after(u, 2))
                if units_left(u, 1):
                    maxima(f, qb, after(u, 1))

            with sp.Fori(0, NB) as b:
                for f, qb in blocks(sp, b, prologue, turn):
                    for i in range(TB):
                        sp.wait_ge(x2_ready, f["tile"] + i + 1)
                        sp.dma_start(out_t[f["tile"] + i], xs[:, i, :]).then_inc(stored, 16)
                    sp.wait_ge(stored, 16 * (f["tile"] + TB))
                    wait_apart(sp, wq_loaded[2], 16 * 3 * (f["block"] + 1))

        @block.gpsimd
        def _(pool):
            c = [0]

            def step(ins):
                c[0] += 1
                ins.then_inc(pool_const, 1)
                pool.wait_ge(pool_const, c[0])

            step(nc.gpsimd.memset(ident[:, :], 0.0))
            step(nc.gpsimd.affine_select(out=ident[:, :], in_=ident[:, :], compare_op=ALU.not_equal, fill=1.0,
                                         base=0, pattern=[[-1, P]], channel_multiplier=1))
            step(nc.gpsimd.tensor_copy(identb[:, :], ident[:, :]))
            step(nc.gpsimd.memset(mask_qk[:, :], 0.0))
            step(nc.gpsimd.affine_select(out=mask_qk[:, :], in_=mask_qk[:, :], compare_op=ALU.is_ge, fill=NEG,
                                         base=0, pattern=[[-1, P]], channel_multiplier=1))
            step(nc.gpsimd.memset(mask_kq[:, :], 0.0))
            step(nc.gpsimd.affine_select(out=mask_kq[:, :], in_=mask_kq[:, :], compare_op=ALU.is_ge, fill=NEG,
                                         base=0, pattern=[[1, P]], channel_multiplier=-1))
            step(nc.gpsimd.memset(ones[:, :], 1.0))
            step(nc.gpsimd.memset(eps_sb[:, :], EPS))
            step(nc.gpsimd.memset(ks[STK:STK + 2, :].bitcast(F32), 1.0))
            for s, n in ((pv_done, CREDIT), (add_pool, CREDIT), (pv_sb, 1), (den_ready, 1)):
                for _ in range(n):
                    nc.gpsimd.memset(scratch[:, 0:1], 0.0).then_inc(s, 1)
                    pool.wait_ge(s, _ + 1)

            def prologue(f, qb):
                pass

            def add(f, qb, u, t):
                sums(pool, nc.gpsimd, add_pool, cp_pool, 0, GH // 2, f, qb, u, t)

            def turn(f, qb, u):
                for v, t in schedule(qb, u):
                    if t >= 2:
                        add(f, qb, v, t - 1)
                    elif t == 0:
                        add(f, qb, u, steps_of(qb) - 1)
                if not units_left(u, 1):
                    add(f, qb, u, steps_of(qb) - 1)

            with pool.Fori(0, NB) as b:
                for f, qb in blocks(pool, b, prologue, turn):
                    wait_apart(pool, ao_ready, f["unit"] + NU)

        @block.scalar
        def _(act):
            act.wait_ge(pool_const, POOL_CONST)
            for n in range(CREDIT):
                nc.scalar.copy(scratch[:, 1:2], eps_sb[:, 0:1]).then_inc(exp_done, 1)
                act.wait_ge(exp_done, n + 1)
            def rough(kind, i):
                L = LN[kind]
                act.wait_ge(L["s_mv"], L["n"] * (i + 1) if L["n"] > 1 else i + 1)
                nc.scalar.activation(L["ln"][:, :], L["mv"][:, :, 1], ACT.Ln, bias=eps_sb[:, 0:1]).then_inc(L["s_ln"], 1)
                act.wait_ge(L["s_ln"], i + 1)
                nc.scalar.activation(L["ex"][:, :], L["ln"][:, :], ACT.Exp, scale=-0.5).then_inc(L["s_ex"], 1)

            def q_part(f, qb, u):
                act.wait_ge(q_ready, unit0(f, u) + 1)
                if not (isinstance(u[0], int) and u[1] == 0):
                    act.wait_ge(qs_loaded[(u[1] - 1) % NP_], filled(f, "stack", after(u, -1)))
                nc.scalar.copy(q1[:, :], ps[:, PQ, :]).then_inc(q1_sb, 1)

            def max_rows(f, qb, u):
                act.wait_ge(mt_ready, unit0(f, u) + 1)
                if not (isinstance(u[0], int) and u[1] == 0):
                    act.wait_ge(qm_loaded[(u[1] - 1) % NP_], filled(f, "rows", after(u, -1)))
                nc.scalar.copy(mT[:, :], ps[0:2 * GH, PAUX, :]).then_inc(mt_sb, 1)

            def exps(f, qb, u, t):
                T = steps_of(qb)
                s = step0(f, qb, u) + t
                c0, _ = cols(qb, t)
                slot = (u[1] * T + t) % NP_
                act.wait_ge(pv_done, CREDIT + s - NP_ + 1)
                a = adds0(f, qb, u) + (max(t - NP_, 1) if t >= NP_ else 1 - NP_ + t)
                act.wait_ge(add_pool, CREDIT + a)
                act.wait_ge(add_dve, CREDIT + a)
                for g in range(GH):
                    act.wait_ge(st_ready, head0(f, qb, u) + GH * t + g + 1)
                    bank = PST + (GH * (u[1] * T + t) + g) % NP_
                    nc.scalar.activation(pr[:, slot, g, c0:], ps[:, bank, c0:], ACT.Exp, scale=SCALE).then_inc(exp_done, 1)

            def pv_copy(f, qb, u):
                act.wait_ge(pv_done, CREDIT + step0(f, qb, u) + steps_of(qb))
                nc.scalar.copy(ao[:, bass.ds(at(u), 1), :], ps[:, PPV:PPV + 1, :]).then_inc(pv_sb, 1)

            def prologue(f, qb):
                rough("pre", f["block"])
                for i in range(TB):
                    act.wait_ge(xt_ready, 2 * (f["tile"] + i) + 1)
                    nc.scalar.copy(xT[:, 0:KT // 2, i * P:(i + 1) * P],
                                   ps[:, PM, :].rearrange("p (k c) -> p k c", c=P)).then_inc(xt_act, 1)
                act.wait_ge(kv_ready, f["block"] + 1)
                nc.scalar.copy(vT[3 * HD:4 * HD, :], ps[3 * HD:4 * HD, PQ, :]).then_inc(k_act, 1)
                nc.scalar.copy(ks[2 * HD:3 * HD, qb * BLK:(qb + 1) * BLK], ps[2 * HD:3 * HD, PQ, :]).then_inc(k_act, 1)
                q_part(f, qb, (0, 0))
                q_part(f, qb, (0, 1))
                max_rows(f, qb, (0, 0))
                for t in range(AHEAD):
                    exps(f, qb, (0, 0), t)

            def turn(f, qb, u):
                T, lead = steps_of(qb), lead_of(qb)
                q_last = max(q_steps(qb))
                for v, t in schedule(qb, u):
                    exps(f, qb, v, t)
                    if v is u and t == q_last and units_left(u, 2):
                        q_part(f, qb, after(u, 2))
                    if v is u and t == T - lead and units_left(u, 1):
                        max_rows(f, qb, after(u, 1))
                    if v is not u and t == 0:
                        pv_copy(f, qb, u)
                if not units_left(u, 1):
                    pv_copy(f, qb, u)

            def post(f, qb):
                base = f["tile"]
                for stage, i in POST:
                    n = base + i
                    if stage == 1:
                        bank = 2 * (i % 2)
                        rough("att", n)
                        act.wait_ge(LN["att"]["s_ch"], CH * (n + 1))
                        for h in range(2):
                            nc.scalar.activation(zs[:, i % 2, h * HALF:(h + 1) * HALF], ps[:, bank + h, :], ACT.Identity,
                                                 scale=LN["att"]["r"][:, 0:1], bias=LN["att"]["nb"][:, 0:1]).then_inc(z1_ready, 1)
                        rough("mid", n)
                    elif stage == 2:
                        act.wait_ge(ht_ready, 2 * n + 1)
                        nc.scalar.copy(xT[:, 0:KT // 2, i * P:(i + 1) * P],
                                       ps[:, 4, :].rearrange("p (k c) -> p k c", c=P)).then_inc(ht_act, 1)
                        act.wait_ge(sm_ch, SM * n + 2)
                        nc.scalar.activation(le[:, i % 2, :], lg[:, i % 2, :], ACT.Exp, bias=nlm[:, i % 2, 0:1]).then_inc(le_ready, 1)
                        act.wait_ge(slt_ready, n + 1)
                        nc.scalar.copy(slT[:, i % 2, :], ps[:, 5, 0:P]).then_inc(slt_sb, 1)
                    else:
                        rough("ffn", n)
                        act.wait_ge(LN["ffn"]["s_ch"], CH * (n + 1))
                        for h in range(2):
                            nc.scalar.activation(zs[:, i % 2, h * HALF:(h + 1) * HALF], ps[:, 7 - h, :], ACT.Identity,
                                                 scale=LN["ffn"]["r"][:, 0:1], bias=LN["ffn"]["nb"][:, 0:1]).then_inc(z2_ready, 1)

            with act.Fori(0, NB) as b:
                for f, qb in blocks(act, b, prologue, turn):
                    post(f, qb)

        @block.vector
        def _(dve):
            dve.wait_ge(pool_const, POOL_CONST)
            c = [0]
            for s, n in ((add_dve, CREDIT), (mx_done, 2), (rden_ready, 1)):
                for _ in range(n):
                    nc.vector.memset(scratch[:, 2:3], 0.0).then_inc(s, 1)
                    dve.wait_ge(s, _ + 1)
            for k in range(WT):
                dve.wait_ge(wt_ready, k + 1)
                bank = k % 4
                if k < KT:
                    nc.vector.tensor_copy(fa_sb[:, k, 0:HR], ps[:, bank, 0:P]).then_inc(wt_read, 1)
                elif k < 2 * KT:
                    nc.vector.tensor_copy(fa_sb[:, k - KT, HR:HR + NF], ps[:, bank, 0:NF]).then_inc(wt_read, 1)
                else:
                    n = k - 2 * KT
                    nc.vector.tensor_copy(fb_sb[:, n * P:(n + 1) * P], ps[:, bank, 0:P]).then_inc(wt_read, 1)

            def stats(kind, n, i, halves):
                L = LN[kind]
                for h, src in enumerate(halves):
                    nc.vector.bn_stats(L["st"][:, i, h, :], src).then_inc(L["s_st"], 1)
                wait_apart(dve, L["s_st"], 2 * (n + 1))
                nc.vector.bn_aggr(L["mv"][:, i, :], L["st"][:, i, :, :]).then_inc(L["s_mv"], 1)

            def newton(kind, n, mv_count):
                L = LN[kind]
                s = L["s_ch"]
                base = CH * n
                dve.wait_ge(L["s_mv"], mv_count)
                nc.vector.tensor_scalar_add(L["ve"][:, :], L["mv"][:, :, 1], EPS).then_inc(s, 1)
                dve.wait_ge(L["s_ex"], n + 1)
                nc.vector.tensor_tensor(L["t1"][:, :], L["ex"][:, :], L["ex"][:, :], ALU.mult).then_inc(s, 1)
                dve.wait_ge(s, base + 2)
                nc.vector.tensor_tensor(L["t2"][:, :], L["t1"][:, :], L["ve"][:, :], ALU.mult).then_inc(s, 1)
                dve.wait_ge(s, base + 3)
                nc.vector.tensor_scalar(L["t3"][:, :], L["t2"][:, :], -0.5, 1.5, ALU.mult, ALU.add).then_inc(s, 1)
                dve.wait_ge(s, base + 4)
                nc.vector.tensor_tensor(L["r"][:, :], L["t3"][:, :], L["ex"][:, :], ALU.mult).then_inc(s, 1)
                dve.wait_ge(s, base + 5)
                nc.vector.scalar_tensor_tensor(out=L["nb"][:, :], in0=L["mv"][:, :, 0], scalar=-1.0, in1=L["r"][:, :],
                                               op0=ALU.mult, op1=ALU.mult).then_inc(s, 1)

            def q_rest(f, qb, u):
                dve.wait_ge(q1_sb, unit0(f, u) + 1)
                if not (isinstance(u[0], int) and u[1] == 0):
                    dve.wait_ge(qs_loaded[(u[1] - 1) % NP_], filled(f, "stack", after(u, -1)))
                nc.vector.tensor_tensor(q2[:, :], ps[:, PQ, :], q1[:, :].bitcast(F32), ALU.subtract).then_inc(q2_sb, 1)

            def maxima(f, qb, u, s):
                c_, qt, n, _ = item(qb, s)
                for g in range(GH):
                    dve.wait_ge(mx_ready, head0(f, qb, u) + GH * s + g + 1)
                    nc.vector.tensor_reduce(mx[:, qt * GH + g, c_:c_ + 1], ps[:, PM + g % 2, 0:n], AX.X,
                                            ALU.max).then_inc(mx_done, 1)
                if s == steps_of(qb) - 1:
                    j = unit0(f, u) + 1
                    dve.wait_ge(mx_done, 2 + head0(f, qb, u) + GH * (s + 1))
                    nc.vector.tensor_reduce(negm[:, :], mx[:, :, 0:qb + 1], AX.X, ALU.max, negate=True).then_inc(negm_ready, 1)
                    dve.wait_ge(negm_ready, j)
                    m_v = negm[:, :].rearrange("p (t g) -> p t g", g=GH)
                    nc.vector.tensor_copy(mz[:, :, :, 0].bitcast(F32R), m_v).then_inc(mz1_ready, 1)
                    dve.wait_ge(mz1_ready, j)
                    nc.vector.tensor_tensor(mz[:, :, :, 1].bitcast(F32R), m_v, mz[:, :, :, 0], ALU.subtract).then_inc(mz_ready, 1)

            def add(f, qb, u, t):
                sums(dve, nc.vector, add_dve, cp_dve, GH // 2, GH, f, qb, u, t)

            def divide(f, qb, u):
                n = unit0(f, u) + 1
                dve.wait_ge(den_ready, 1 + n)
                nc.vector.reciprocal(rden[:, :], ps[:, PAUX, :]).then_inc(rden_ready, 1)
                dve.wait_ge(rden_ready, 1 + n)
                dve.wait_ge(pv_sb, 1 + n)
                a = ao[:, bass.ds(at(u), 1), :]
                nc.vector.tensor_tensor(a, a, rden[:, None, :], ALU.mult).then_inc(ao_ready, 1)

            def prologue(f, qb):
                base = f["tile"]
                for i in range(TB):
                    dve.wait_ge(x_loaded[i], 16 * (f["block"] + 1))
                    stats("pre", base + i, i, [xs[:, i, h * HALF:(h + 1) * HALF] for h in range(2)])
                newton("pre", f["block"], base + TB)
                dve.wait_ge(LN["pre"]["s_ch"], CH * (f["block"] + 1))

                def xt_copy(i):
                    dve.wait_ge(xt_ready, 2 * (base + i) + 2)
                    nc.vector.tensor_copy(xT[:, KT // 2:KT, i * P:(i + 1) * P],
                                          ps[:, PM + 1, :].rearrange("p (k c) -> p k c", c=P)).then_inc(xt_dve, 1)
                for i in range(TB):
                    nc.vector.tensor_scalar(xn[:, i % 2, :], xs[:, i, :], LN["pre"]["mv"][:, i, 0:1], LN["pre"]["r"][:, i:i + 1],
                                            ALU.subtract, ALU.mult).then_inc(xn_ready, 1)
                    if i >= 1:
                        xt_copy(i - 1)
                xt_copy(TB - 1)
                here = slice(qb * BLK, (qb + 1) * BLK)
                nb_ = f["block"]
                dve.wait_ge(kv_ready, nb_ + 1)
                nc.vector.tensor_copy(k1t[HD:2 * HD, :], ps[HD:2 * HD, PQ, :]).then_inc(k_dve, 1)
                nc.vector.tensor_copy(ks[0:HD, here], ps[0:HD, PQ, :]).then_inc(k_dve, 1)
                dve.wait_ge(k_dve, 3 * nb_ + 1)
                nc.vector.tensor_tensor(ks[HD:2 * HD, here], ps[HD:2 * HD, PQ, :], k1t[HD:2 * HD, :].bitcast(F32),
                                        ALU.subtract).then_inc(k_dve, 1)
                dve.wait_ge(v_tr, nb_ + 1)
                nc.vector.tensor_copy(vs[:, TB * qb:TB * (qb + 1), :],
                                      ps[:, PAUX, 0:TB * HD].rearrange("p (t d) -> p t d", d=HD)).then_inc(v_sb, 1)
                q_rest(f, qb, (0, 0))
                q_rest(f, qb, (0, 1))
                for s in range(steps_of(qb)):
                    maxima(f, qb, (0, 0), s)
                for s in range(lead_of(qb)):
                    maxima(f, qb, (0, 1), s)
                for t in range(AHEAD):
                    maxima(f, qb, *normal(qb, (0, 1), t + lead_of(qb)))

            def turn(f, qb, u):
                T, lead = steps_of(qb), lead_of(qb)
                q_last = max(q_steps(qb))
                for v, t in schedule(qb, u):
                    w, s = normal(qb, after(v, 1), t + lead)
                    if not isinstance(w[0], int) or w[1] < NU:
                        maxima(f, qb, w, s)
                    if v is u and t == q_last and units_left(u, 2):
                        q_rest(f, qb, after(u, 2))
                    if t >= 2:
                        add(f, qb, v, t - 1)
                    elif t == 0:
                        add(f, qb, u, T - 1)
                if not units_left(u, 1):
                    add(f, qb, u, T - 1)
                divide(f, qb, u)

            def post(f, qb):
                base = f["tile"]
                for stage, i in POST:
                    n = base + i
                    if stage == 1:
                        bank = 2 * (i % 2)
                        dve.wait_ge(y1_ready, n + 1)
                        stats("att", n, 0, [ps[:, bank, :], ps[:, bank + 1, :]])
                        newton("att", n, n + 1)
                        dve.wait_ge(z1_ready, 2 * n + 2)
                        nc.vector.tensor_tensor(xs[:, i, :], xs[:, i, :], zs[:, i % 2, :], ALU.add).then_inc(x1_ready, 1)
                        dve.wait_ge(x1_ready, n + 1)
                        stats("mid", n, 0, [xs[:, i, h * HALF:(h + 1) * HALF] for h in range(2)])
                        newton("mid", n, n + 1)
                        dve.wait_ge(LN["mid"]["s_ch"], CH * (n + 1))
                        if i >= 2:
                            dve.wait_ge(ht_ready, 2 * (n - 2) + 2)
                        nc.vector.tensor_scalar(xn[:, i % 2, :], xs[:, i, :], LN["mid"]["mv"][:, 0, 0:1], LN["mid"]["r"][:, 0:1],
                                                ALU.subtract, ALU.mult).then_inc(h_ready, 1)
                    elif stage == 2:
                        dve.wait_ge(ht_ready, 2 * n + 2)
                        nc.vector.tensor_copy(xT[:, KT // 2:KT, i * P:(i + 1) * P],
                                              ps[:, 5, :].rearrange("p (k c) -> p k c", c=P)).then_inc(ht_dve, 1)
                        dve.wait_ge(low_ready, n + 1)
                        k = i % 2
                        m = SM * n
                        nc.vector.tensor_tensor(lg[:, k, :], ps[:, 6, HR:HR + NF], br_sb[:, :], ALU.add).then_inc(sm_ch, 1)
                        dve.wait_ge(sm_ch, m + 1)
                        nc.vector.tensor_reduce(nlm[:, k, :], lg[:, k, :], AX.X, ALU.max, negate=True).then_inc(sm_ch, 1)
                        dve.wait_ge(le_ready, n + 1)
                        nc.vector.tensor_reduce(ls[:, k, :], le[:, k, :], AX.X, ALU.add).then_inc(sm_ch, 1)
                        dve.wait_ge(sm_ch, m + 3)
                        nc.vector.reciprocal(lr[:, k, :], ls[:, k, :]).then_inc(sm_ch, 1)
                        dve.wait_ge(sm_ch, m + 4)
                        nc.vector.tensor_scalar(lw[:, k, :], le[:, k, :], lr[:, k, 0:1], NF * SCALING, ALU.mult, ALU.mult).then_inc(sm_ch, 1)
                        dve.wait_ge(sm_ch, m + 5)
                        nc.vector.tensor_tensor(sl[:, k, :].rearrange("p (h r) -> p h r", h=NF),
                                                ps[:, 6, 0:HR].rearrange("p (h r) -> p h r", h=NF),
                                                lw[:, k, :, None].to_broadcast([P, NF, RANK]), ALU.mult).then_inc(sl_ready, 1)
                    else:
                        dve.wait_ge(y2_ready, n + 1)
                        stats("ffn", n, 0, [ps[:, 7, :], ps[:, 6, :]])
                        newton("ffn", n, n + 1)
                        dve.wait_ge(z2_ready, 2 * n + 2)
                        nc.vector.tensor_tensor(xs[:, i, :], xs[:, i, :], zs[:, i % 2, :], ALU.add).then_inc(x2_ready, 1)

            with dve.Fori(0, NB) as b:
                for f, qb in blocks(dve, b, prologue, turn):
                    post(f, qb)

        @block.tensor
        def _(pe):
            pe.wait_ge(pool_const, POOL_CONST)
            pe.wait_ge(const_loaded, 16 * N_CONST)
            for k in range(WT):
                bank = k % 4
                if k >= 4:
                    pe.wait_ge(wt_read, k - 3)
                if k < KT:
                    nc.tensor.transpose(ps[:, bank, 0:P], xs[:, 0, k * P:(k + 1) * P], ident[:, :]).then_inc(wt_ready, 1)
                elif k < 2 * KT:
                    n = k - KT
                    nc.tensor.transpose(ps[:, bank, 0:NF], xs[0:NF, 1, n * P:(n + 1) * P], ident[0:NF, 0:NF]).then_inc(wt_ready, 1)
                else:
                    n = k - 2 * KT
                    nc.tensor.transpose(ps[:, bank, 0:P], xs[:, 2, n * P:(n + 1) * P], ident[:, :]).then_inc(wt_ready, 1)
            pe.wait_ge(wt_read, WT)

            def project(f, qb, u, tiles):
                if 0 in tiles:
                    pe.wait_ge(wq_loaded[u[1] % NP_], f["wq"] + 16 * (u[1] // NP_ + 1))
                    if not (isinstance(u[0], int) and u[1] == 0):
                        pe.wait_ge(q1_sb, unit0(f, u))
                        pe.wait_ge(q2_sb, unit0(f, u))
                for k in tiles:
                    last = nc.tensor.matmul(ps[:, PQ, :], wq_sb[:, u[1] % NP_, k, :], xT[:, k, :],
                                            start=(k == 0), stop=(k == KT - 1))
                if KT - 1 in tiles:
                    last.then_inc(q_ready, 1)

            def max_scores(f, qb, u, s, g):
                c, qt, n, diagonal = item(qb, s)
                if s == 0 and g == 0:
                    pe.wait_ge(qs_loaded[u[1] % NP_], filled(f, "stack", u))
                pe.wait_ge(mx_done, 2 + head0(f, qb, u) + GH * s + g - 1)
                bank = PM + g % 2
                last = nc.tensor.matmul(ps[:, bank, 0:n], qs[0:STK, u[1] % NP_, g, qt * P:(qt + 1) * P],
                                        ks[0:STK, c * BLK:c * BLK + n], start=True, stop=not diagonal)
                if diagonal:
                    last = nc.tensor.matmul(ps[:, bank, n - P:n], identb[:, :], mask_qk[:, :], start=False, stop=True)
                last.then_inc(mx_ready, 1)

            def scores(f, qb, u, t, g):
                T = steps_of(qb)
                c0, diagonal = cols(qb, t)
                if t == 0 and g == 0:
                    pe.wait_ge(qm_loaded[u[1] % NP_], filled(f, "rows", u))
                n = head0(f, qb, u) + GH * t + g
                bank = PST + (GH * (u[1] * T + t) + g) % NP_
                pe.wait_ge(exp_done, CREDIT + n - NP_ + 1)
                last = nc.tensor.matmul(ps[:, bank, c0:], ks[0:STK + 2, t * P:(t + 1) * P],
                                        qs[0:STK + 2, u[1] % NP_, g, c0:], start=True, stop=not diagonal)
                if diagonal:
                    last = nc.tensor.matmul(ps[:, bank, c0:c0 + P], identb[:, :], mask_kq[:, :], start=False, stop=True)
                last.then_inc(st_ready, 1)

            def values(f, qb, u, t):
                T = steps_of(qb)
                c0, _ = cols(qb, t)
                if t == 0:
                    pe.wait_ge(pv_sb, 1 + unit0(f, u))
                for g in range(GH):
                    pe.wait_ge(exp_done, CREDIT + head0(f, qb, u) + GH * t + g + 1)
                    last = nc.tensor.matmul(ps[g * HD:(g + 1) * HD, PPV, c0:], vs[:, t, :], pr[:, (u[1] * T + t) % NP_, g, c0:],
                                            start=(t == 0), stop=(t == T - 1))
                last.then_inc(pv_done, 1)

            def max_transposes(f, qb, u):
                pe.wait_ge(mz_ready, unit0(f, u) + 1)
                if not (isinstance(u[0], int) and u[1] == 0):
                    pe.wait_ge(rden_ready, 1 + unit0(f, u) - 1)
                for qt in range(TB):
                    last = nc.tensor.transpose(ps[0:2 * GH, PAUX, qt * P:(qt + 1) * P],
                                               mz[:, qt, :, :].rearrange("p g c -> p (g c)"), ident[:, :])
                last.then_inc(mt_ready, 1)

            def sum_keys(f, qb, u):
                n = adds0(f, qb, u) + steps_of(qb) - 1
                pe.wait_ge(add_pool, CREDIT + n)
                pe.wait_ge(add_dve, CREDIT + n)
                if units_left(u, 1):
                    pe.wait_ge(mt_sb, unit0(f, u) + 2)
                for g in range(GH):
                    last = nc.tensor.matmul(ps[g * HD:(g + 1) * HD, PAUX, :], ones[:, :], ds[:, g, :], start=True, stop=True)
                last.then_inc(den_ready, 1)

            def step(f, qb, u, t, prev):
                w, s = normal(qb, after(u, 1), t + lead_of(qb))
                more = not isinstance(w[0], int) or w[1] < NU
                for g in range(GH):
                    scores(f, qb, u, t, g)
                    if more:
                        max_scores(f, qb, w, s, g)
                if t >= 1:
                    values(f, qb, u, t - 1)
                elif prev is not None:
                    values(f, qb, prev, steps_of(qb) - 1)

            def prologue(f, qb):
                base = f["tile"]
                for i in range(TB):
                    pe.wait_ge(xn_ready, base + i + 1)
                    for h in range(2):
                        if i >= 1:
                            pe.wait_ge((xt_act, xt_dve)[h], base + i)
                        for k in range(KT // 2):
                            kk = h * KT // 2 + k
                            last = nc.tensor.transpose(ps[:, PM + h, k * P:(k + 1) * P], xn[:, i % 2, kk * P:(kk + 1) * P], ident[:, :])
                        last.then_inc(xt_ready, 1)
                pe.wait_ge(xt_act, base + TB)
                pe.wait_ge(xt_dve, base + TB)
                for k in range(KT):
                    last = nc.tensor.matmul(ps[:, PQ, :], wkv_sb[:, k, :], xT[:, k, :], start=(k == 0), stop=(k == KT - 1))
                last.then_inc(kv_ready, 1)
                n = f["block"] + 1
                wait_apart(pe, k_act, 2 * n)
                for i in range(TB):
                    last = nc.tensor.transpose(ps[:, PAUX, i * HD:(i + 1) * HD], vT[3 * HD:4 * HD, i * P:(i + 1) * P],
                                               ident[3 * HD:4 * HD, 3 * HD:4 * HD])
                last.then_inc(v_tr, 1)
                pe.wait_ge(k_dve, 3 * n)
                project(f, qb, (0, 0), range(KT))
                project(f, qb, (0, 1), range(KT))
                for s in range(steps_of(qb)):
                    for g in range(GH):
                        max_scores(f, qb, (0, 0), s, g)
                for s in range(lead_of(qb)):
                    for g in range(GH):
                        max_scores(f, qb, (0, 1), s, g)
                pe.wait_ge(v_sb, n)
                max_transposes(f, qb, (0, 0))
                for t in range(AHEAD):
                    step(f, qb, (0, 0), t, None)

            def turn(f, qb, u):
                T, lead = steps_of(qb), lead_of(qb)
                q_at = q_steps(qb)
                for v, t in schedule(qb, u):
                    if v is u and t in q_at and units_left(u, 2):
                        project(f, qb, after(u, 2), q_at[t])
                    step(f, qb, v, t, u)
                    if v is u and t == T - lead and units_left(u, 1):
                        max_transposes(f, qb, after(u, 1))
                if not units_left(u, 1):
                    values(f, qb, u, T - 1)
                sum_keys(f, qb, u)

            def post(f, qb):
                base = f["tile"]
                pe.wait_ge(ao_ready, f["unit"] + NU)
                for stage, i in POST_PE:
                    n = base + i
                    if stage == 1:
                        if i >= 2:
                            pe.wait_ge(z1_ready, 2 * (n - 2) + 2)
                        for h in range(2):
                            for k in range(KT):
                                last = nc.tensor.matmul(ps[:, 2 * (i % 2) + h, :], ao[:, k, i * P:(i + 1) * P],
                                                        wo_sb[:, k, h * HALF:(h + 1) * HALF], start=(k == 0), stop=(k == KT - 1))
                        last.then_inc(y1_ready, 1)
                    elif stage == 2:
                        pe.wait_ge(h_ready, n + 1)
                        if i >= 1:
                            pe.wait_ge(ht_act, n)
                            pe.wait_ge(ht_dve, n)
                            pe.wait_ge(slt_sb, n)
                        for h in range(2):
                            for k in range(KT // 2):
                                kk = h * KT // 2 + k
                                last = nc.tensor.transpose(ps[:, 4 + h, k * P:(k + 1) * P], xn[:, i % 2, kk * P:(kk + 1) * P], ident[:, :])
                            last.then_inc(ht_ready, 1)
                        pe.wait_ge(ht_act, n + 1)
                        pe.wait_ge(ht_dve, n + 1)
                        if i >= 1:
                            pe.wait_ge(z2_ready, 2 * (n - 1) + 2)
                        for k in range(KT):
                            last = nc.tensor.matmul(ps[:, 6, 0:HR + NF], xT[:, k, i * P:(i + 1) * P], fa_sb[:, k, :],
                                                    start=(k == 0), stop=(k == KT - 1))
                        last.then_inc(low_ready, 1)
                    else:
                        pe.wait_ge(sl_ready, n + 1)
                        nc.tensor.transpose(ps[:, 5, 0:P], sl[:, i % 2, :], ident[:, :]).then_inc(slt_ready, 1)
                        pe.wait_ge(slt_sb, n + 1)
                        for h in range(2):
                            last = nc.tensor.matmul(ps[:, 7 - h, :], slT[:, i % 2, :], fb_sb[:, h * HALF:(h + 1) * HALF],
                                                    start=True, stop=True)
                        last.then_inc(y2_ready, 1)
                pe.wait_ge(z2_ready, 2 * (base + TB))

            with pe.Fori(0, NB) as b:
                for f, qb in blocks(pe, b, prologue, turn):
                    post(f, qb)


_INS = ['L0_attn_x', 'L0_attn_wq', 'L0_attn_wk', 'L0_attn_wv', 'L0_attn_wo', 'L0_ffn_A', 'L0_ffn_B', 'L0_ffn_Wr', 'L0_ffn_br']


def kernel(**inputs):
    import numpy as _np
    import concourse.bacc as _bacc
    from concourse import mybir as _mybir
    from concourse.bass_utils import run_bass_kernel_spmd as _run

    nc = _bacc.Bacc("TRN2", target_bir_lowering=False, num_devices=1)
    arrays, args = {}, []
    for name in _INS:
        a = _np.ascontiguousarray(inputs[name])
        arrays[f"in_{name}_dram"] = a
        args.append(nc.dram_tensor(f"in_{name}_dram", a.shape, _mybir.dt.from_np(a.dtype), kind="ExternalInput").ap())
    shape = tuple(inputs["L0_attn_x"].shape)
    args.append(nc.dram_tensor("out_0_dram", shape, _mybir.dt.from_np(_np.dtype("float32")), kind="ExternalOutput").ap())
    bass_mqa_sandwich_lora_router(nc, *args)
    r = _run(nc, [arrays], core_ids=[0])
    return r.results[0]["out_0_dram"]
```

```python
import concourse.bass as bass
from concourse import mybir
from contextlib import ExitStack


def bass_mqa_sandwich_lora_router(nc, x, wq, wk, wv, wo, ffn_a, ffn_b, ffn_wr, ffn_br, out):
    F32, F32R, BF16, I32 = mybir.dt.float32, mybir.dt.float32r, mybir.dt.bfloat16, mybir.dt.int32
    ALU, ACT, AX = mybir.AluOpType, mybir.ActivationFunctionType, mybir.AxisListType

    P = 128
    NB, NT, D = x.shape
    HD = wk.shape[1]
    NH = wq.shape[1] // HD
    GH = P // HD
    NU = NH // GH
    KT = D // P
    BLK = 512
    TB = BLK // P
    NQ = NT // BLK
    HALF = 512
    NF, RANK, _ = ffn_a.shape
    HR = NF * RANK
    SCALE = float(HD) ** -0.5
    SCALING = 32.0 / RANK
    EPS = 1e-5
    NEG = -1e30
    ROUNDS = 3
    MAGIC = 0x5F3759DF
    STK = 3 * HD
    NP_ = 3

    def steps_of(qb):
        return TB * (qb + 1)

    STEPS = NU * sum(steps_of(q) for q in range(NQ))

    def base_counts(b, qb, r):
        T, blk = steps_of(qb), b * NQ + qb
        step = b * STEPS + NU * sum(steps_of(q) for q in range(qb)) + r * (NP_ * T)
        unit = b * (NQ * NU) + qb * NU + r * NP_
        return dict(
            block=blk, tile=blk * TB, unit=unit,
            step=step, step4=step * GH,
            add=b * (STEPS - NQ * NU) + NU * sum(steps_of(q) - 1 for q in range(qb)) + r * (NP_ * (T - 1)),
            unit_of_first=b * NU + r * NP_,
            wq=blk * (16 * NP_) + r * 16,
            **{f"{name}{n}": blk * (d * n) + r * d
               for name, d in (("stack", 16 * 3 * GH), ("rows", 16 * GH)) for n in set(UNITS_OF_SLOT)})

    UNITS_OF_SLOT = [len(range(i, NU, NP_)) for i in range(NP_)]

    def frame(engine, b, qb, r):
        return dict(b=b, r=r, **{k: engine.snap(v) for k, v in base_counts(b, qb, r).items()})

    def unit0(f, u):
        return f["unit"] + u[1]

    def step0(f, qb, u):
        return f["step"] + u[1] * steps_of(qb)

    def head0(f, qb, u):
        return f["step4"] + GH * u[1] * steps_of(qb)

    def adds0(f, qb, u):
        return f["add"] + u[1] * (steps_of(qb) - 1)

    def filled(f, name, u):
        d = 16 * 3 * GH if name == "stack" else 16 * GH
        return f[f"{name}{UNITS_OF_SLOT[u[1] % NP_]}"] + d * (u[1] // NP_ + 1)

    def lead_of(qb):
        return max(1, steps_of(qb) // 4)

    def reach(qb):
        return 3 if steps_of(qb) == TB else 2

    x_t = x.rearrange("b (n p) d -> (b n) p d", p=P)
    out_t = out.rearrange("b (n p) d -> (b n) p d", p=P)
    wq_v = wq.rearrange("(k p) m -> p k m", p=P)
    wo_v = wo.rearrange("(k p) m -> p k m", p=P)
    wk_v = wk.rearrange("(k p) m -> p k m", p=P)
    wv_v = wv.rearrange("(k p) m -> p k m", p=P)
    fb_v = ffn_b.rearrange("h (n p) r -> n p h r", p=P)

    ctx = ExitStack()
    with ctx:
        def sb(name, shape, dt=F32):
            return ctx.enter_context(nc.sbuf_tensor(name, shape, dt))

        def sem(name):
            return ctx.enter_context(nc.semaphore(name))

        wo_sb = sb("wo_sb", [P, KT, D])
        wkv_sb = sb("wkv_sb", [P, KT, 4 * HD])
        wq_sb = sb("wq_sb", [P, 3, KT, P])
        fa_sb = sb("fa_sb", [P, KT, HR + NF])
        fb_sb = sb("fb_sb", [HR, D])
        br_sb = sb("br_sb", [P, NF])
        ident = sb("ident", [P, P])
        identb = sb("identb", [P, P], BF16)
        mask_qk = sb("mask_qk", [P, P], BF16)
        mask_kq = sb("mask_kq", [P, P], BF16)
        ones = sb("ones", [P, HD])
        eps_sb = sb("eps_sb", [P, 1])
        xs = sb("xs", [P, TB, D])
        t4 = sb("t4", [P, TB, D])
        zs = t4
        xT = sb("xT", [P, KT, BLK])
        ks = sb("ks", [P, NT], F32R)
        kv = sb("kv", [P, BLK])
        vs = sb("vs", [P, NT // P, HD])
        q1 = sb("q1", [P, BLK], F32R)
        q2 = sb("q2", [P, BLK], F32R)
        qs = sb("qs", [P, NP_, GH, BLK], F32R)
        mx = sb("mx", [P, TB * GH, NQ])
        negm = sb("negm", [P, TB * GH])
        mz = sb("mz", [P, TB, GH, 2])
        mT = sb("mT", [2 * GH, BLK], F32R)
        pr = sb("pr", [P, NP_, GH, BLK])
        xn = pr[:, 0:2, :, :].rearrange("p s (j g) c -> p (s j) (g c)", j=2)
        hT = pr[:, 2, :, :].rearrange("p (i h) (k c) -> p i (h k) c", i=2, c=P)
        ds = sb("ds", [P, GH, BLK])
        rden = sb("rden", [P, BLK])
        ao = sb("ao", [P, NU, BLK])
        scratch = sb("scratch", [P, 4])
        m1 = sb("m1", [P, TB])
        sh = sb("sh", [P, 2, 2])
        lg = sb("lg", [P, 2, NF])
        nlm = sb("nlm", [P, 2, 1])
        le = sb("le", [P, 2, NF])
        ls = sb("ls", [P, 2, 1])
        lr = sb("lr", [P, 2, 1])
        lw = sb("lw", [P, 2, NF])
        sl = sb("sl", [P, 2, HR])
        slT = sb("slT", [P, 2, P])
        LN = {}
        for kind, n in (("pre", TB), ("att", 1), ("mid", 1), ("ffn", 1)):
            LN[kind] = dict(
                n=n, st=sb(f"st_{kind}", [P, n, 2, 6]), mv=sb(f"mv_{kind}", [P, n, 2]), ve=sb(f"ve_{kind}", [P, n]),
                half=sb(f"half_{kind}", [P, n], I32), y0=sb(f"y0_{kind}", [P, n], I32), y=sb(f"y_{kind}", [P, ROUNDS, n]),
                a=sb(f"a_{kind}", [P, ROUNDS, n]), c=sb(f"c_{kind}", [P, ROUNDS, n]),
                r=sb(f"r_{kind}", [P, n]),
                s_st=sem(f"{kind}_stats"), s_mv=sem(f"{kind}_meanvar"), s_ch=sem(f"{kind}_rsqrt"))

        ps = ctx.enter_context(nc.psum_tensor("ps", [P, 8, HALF], F32))
        PM, PST, PPV, PQ, PAUX = 0, 3, 5, 6, 7
        PY = 2

        def CH(kind):
            return 4 + (3 * ROUNDS if LN[kind]["n"] > 1 else 3 * ROUNDS - 1)

        def pair(i):
            return 4 + 2 * (i % 2)

        const_loaded = sem("const_loaded")
        pool_const = sem("pool_const")
        wt_ready = sem("wt_ready")
        wt_read = sem("wt_read")
        x_loaded = [sem(f"x_loaded{i}") for i in range(TB)]
        r_loaded = [sem(f"r_loaded{i}") for i in range(TB)]
        wq_loaded = [sem(f"wq_loaded{i}") for i in range(3)]
        xn_ready = sem("xn_ready")
        xt_ready = sem("xt_ready")
        xt_act = sem("xt_act")
        xt_dve = sem("xt_dve")
        kv_ready = sem("kv_ready")
        k_act = sem("k_act")
        k_dve = sem("k_dve")
        v_tr = sem("v_tr")
        v_sb = sem("v_sb")
        q_ready = sem("q_ready")
        q1_sb = sem("q1_sb")
        q2_sb = sem("q2_sb")
        qs_loaded = [sem(f"qs_loaded{i}") for i in range(NP_)]
        mx_ready = sem("mx_ready")
        mx_done = sem("mx_done")
        negm_ready = sem("negm_ready")
        mz1_ready = sem("mz1_ready")
        mz_ready = sem("mz_ready")
        mt_ready = sem("mt_ready")
        mt_sb = sem("mt_sb")
        qm_loaded = [sem(f"qm_loaded{i}") for i in range(NP_)]
        st_ready = sem("st_ready")
        exp_done = sem("exp_done")
        pv_done = sem("pv_done")
        pv_sb = sem("pv_sb")
        add_pool = sem("add_pool")
        add_dve = sem("add_dve")
        cp_pool = sem("cp_pool")
        cp_dve = sem("cp_dve")
        den_ready = sem("den_ready")
        rden_ready = sem("rden_ready")
        ao_ready = sem("ao_ready")
        y1_ready = sem("y1_ready")
        z1_ready = sem("z1_ready")
        x1_ready = sem("x1_ready")
        m1_ready = sem("m1_ready")
        h_ready = sem("h_ready")
        sh_ready = sem("sh_ready")
        ht_ready = sem("ht_ready")
        ht_sb = sem("ht_sb")
        low_ready = sem("low_ready")
        sm_ch = sem("sm_ch")
        le_ready = sem("le_ready")
        sl_ready = sem("sl_ready")
        slt_ready = sem("slt_ready")
        slt_sb = sem("slt_sb")
        y2_ready = sem("y2_ready")
        z2_ready = sem("z2_ready")
        x2_ready = sem("x2_ready")
        stored = sem("stored")
        passed = sem("passed")

        nc.disable_value_cache = True
        block = ctx.enter_context(nc.Block())

        CREDIT = 3
        AHEAD = 2

        def at(u):
            return u[0] * NP_ + u[1]

        def after(u, n):
            return (u[0], u[1] + n)

        def cols(qb, t):
            return (t - TB * qb) * P if t >= TB * qb else 0, t >= TB * qb

        def item(qb, s):
            c, qt = s // TB, s % TB
            return c, qt, (qt + 1) * P if c == qb else BLK, c == qb

        def is_early(qb, u, s):
            return u[1] == 0 or (u[1] == 1 and s < lead_of(qb))

        def first_of_three(qb, u, s, g):
            return u[1] == 1 and 0 <= GH * (s - lead_of(qb)) + g < NP_

        def mx_bank(qb, u, s, g):
            return PM + (g % 2 if is_early(qb, u, s) else (GH * (u[1] * steps_of(qb) + s) + g) % NP_)

        def rows_bank(qb, u):
            return PQ if reach(qb) > 2 and u[1] > 0 else PAUX

        def normal(qb, u, t):
            return (u, t) if t < steps_of(qb) else (after(u, 1), t - steps_of(qb))

        def schedule(qb, u):
            T, n = steps_of(qb), u[1] if isinstance(u[0], int) else None
            last = n == NU - 1
            return [(u, t) for t in range(AHEAD, T)] + ([] if last else [(after(u, 1), t) for t in range(AHEAD)])

        def static_unit(u):
            return u[1] if isinstance(u[0], int) else None

        def units_left(u, n):
            j = static_unit(u)
            return j is None or j + n < NU

        def blocks(engine, b, prologue, turn):
            for qb in range(NQ):
                f = frame(engine, b, qb, 0)
                prologue(f, qb)
                if reach(qb) == 2:
                    with engine.Fori(0, (NU - 2) // NP_) as r:
                        g = frame(engine, b, qb, r)
                        for k in range(NP_):
                            turn(g, qb, (r, k), None)
                    f = frame(engine, b, qb, 0)
                else:
                    for k in range(NU - 2):
                        turn(f, qb, (0, k), None)
                nf = frame(engine, b, qb + 1, 0) if opens(qb) else None
                turn(f, qb, (0, NU - 2), nf)
                turn(f, qb, (0, NU - 1), nf)
                yield f, qb, nf

        def q_steps(qb):
            if reach(qb) > 2:
                return {steps_of(qb) - 1: range(KT)}
            n = max(1, steps_of(qb) // 2 - 3)
            per = -(-KT // n)
            return {AHEAD + i: range(i * per, min(KT, (i + 1) * per)) for i in range(n) if i * per < KT}

        END = -1

        def opening(qb):
            T = steps_of(qb)
            if T == TB:
                return {2: [("tr", 0), ("tr", 1)], 3: [("tr", 2), ("tr", 3)], END: [("kv", 0), ("vt", 0), ("q", 0)]}
            plan = {2 + i: [("tr", i)] for i in range(TB)}
            if T == 2 * TB:
                return {**plan, 7: [("kv", 0)], END: [("vt", 0), ("q", 0)]}
            return {**plan, 7: [("kv", 0)], 9: [("vt", 0)], 10: [("q", 0)]}

        def opens(qb):
            return qb + 1 < NQ

        def early_items(qb):
            return [((0, 0), s) for s in range(steps_of(qb))] + [((0, 1), s) for s in range(lead_of(qb))]

        def stages(text):
            return [(w.rstrip("0123456789"), int(w.lstrip("abcdefghijklmnopqrstuvwxyz"))) for w in text.split()]

        CLOSE_PE = stages("""proj0 max0 proj1 max1 proj2 max2 proj3 max3 proj4 proj5 proj6 proj7 max4 proj8 proj9 proj10 proj11
                             max5 turn0 max6 low0 proj12 proj13 up0 proj14 proj15 max7 turn1 max8 low1 up1 turn2 low2 max9
                             up2 rows0 turn3 max10 low3 max11 up3""")
        CLOSE_DVE = stages("""max0 max1 max2 max3 proj0 max4 proj1 max5 max6 low0 proj2 sum0 max7 max8 low1 proj3 sum1 low2 max9
                              sum2 max10 low3 max11 sum3""")
        CLOSE_ACT = stages("""proj0 proj1 proj2 turn0 low0 up0 proj3 sum0 turn1 low1 up1 turn2 sum1 low2 up2 rows0 sum2 turn3 low3
                              up3 exps0 sum3""")
        PORTIONS = 12

        def portion(qb, k):
            if not opens(qb):
                return []
            every = early_items(qb + 1)
            first = TB + 2
            if k < TB:
                return every[first * k // TB:first * (k + 1) // TB]
            n, k, m = len(every) - first, k - TB, PORTIONS - TB
            return every[first + n * k // m:first + n * (k + 1) // m]

        N_CONST = 3 + 1 + 1 + 1 + 1 + 1 + D // P

        def wait_apart(engine, s, value):
            engine.wait_ge(s, value)
            engine.sem_inc(passed, 1)

        def pool_heads(qb, u):
            return GH - 1 if qb >= 2 else GH // 2

        def sums(engine, ops, added, copied, g0, g1, f, qb, u, t):
            T = steps_of(qb)
            c0, _ = cols(qb, t)
            engine.wait_ge(exp_done, CREDIT + head0(f, qb, u) + GH * t + g1)
            this = pr[:, (u[1] * T + t) % NP_, g0:g1, c0:]
            if t == 1:
                wait_apart(engine, den_ready, 1 + unit0(f, u))
                first = pr[:, (u[1] * T) % NP_, g0:g1, :]
                if c0:
                    ops.tensor_copy(ds[:, g0:g1, 0:c0], first[:, :, 0:c0]).then_inc(copied, 1)
                    engine.wait_ge(copied, f["unit_of_first"] + u[1] + 1)
                ops.tensor_tensor(ds[:, g0:g1, c0:], first[:, :, c0:], this, ALU.add).then_inc(added, 1)
            else:
                engine.wait_ge(added, CREDIT + adds0(f, qb, u) + t - 1)
                ops.tensor_tensor(ds[:, g0:g1, c0:], ds[:, g0:g1, c0:], this, ALU.add).then_inc(added, 1)

        WT = 3 * KT
        POOL_CONST = 10
        SM = 5

        @block.sync
        def _(sp):
            for c in range(3):
                sp.dma_start(wkv_sb[:, :, c * HD:(c + 1) * HD], wk_v).then_inc(const_loaded, 16)
            sp.dma_start(wkv_sb[:, :, 3 * HD:4 * HD], wv_v).then_inc(const_loaded, 16)
            sp.dma_start(wo_sb[:, :, :], wo_v).then_inc(const_loaded, 16)
            sp.dma_start(xs[:, 0, :], ffn_a.rearrange("h r d -> (h r) d")).then_inc(const_loaded, 16)
            sp.dma_start(xs[0:NF, 1, :], ffn_wr).then_inc(const_loaded, 16)
            sp.dma_start(br_sb[:, :], ffn_br.partition_broadcast(P)).then_inc(const_loaded, 16)
            for n in range(D // P):
                sp.dma_start(xs[:, 2, n * P:(n + 1) * P].rearrange("p (h r) -> p h r", h=NF),
                             fb_v[n]).then_inc(const_loaded, 16)
            sp.wait_ge(wt_read, WT)

            def load_wq(j, slot):
                sp.dma_start(wq_sb[:, slot, :, :], wq_v[:, :, bass.ds(j * P, P)]).then_inc(wq_loaded[slot], 16)

            def stack(f, qb, u):
                n = unit0(f, u) + 1
                sp.wait_ge(q1_sb, n)
                sp.wait_ge(q2_sb, n)
                slot = u[1] % NP_
                for g in range(GH):
                    for row, part in ((0, q1), (HD, q1), (2 * HD, q2)):
                        sp.dma_start(qs[row:row + HD, slot, g, :].bitcast(F32),
                                     part[g * HD:(g + 1) * HD, :].bitcast(F32)).then_inc(qs_loaded[slot], 16)

            def maxima(f, qb, u):
                sp.wait_ge(mt_sb, unit0(f, u) + 1)
                slot = u[1] % NP_
                for g in range(GH):
                    sp.dma_start(qs[STK:STK + 2, slot, g, :].bitcast(F32),
                                 mT[2 * g:2 * g + 2, :].bitcast(F32)).then_inc(qm_loaded[slot], 16)

            def tokens(f, qb):
                for i in range(TB):
                    sp.dma_start(t4[:, i, :], x_t[f["tile"] + i]).then_inc(x_loaded[i], 16)

            def prologue(f, qb):
                if qb == 0:
                    tokens(f, qb)
                    for j in range(3):
                        load_wq(j, j)
                for i in range(TB):
                    sp.dma_start(xs[:, i, :], x_t[f["tile"] + i]).then_inc(r_loaded[i], 16)
                if qb == 0:
                    sp.wait_ge(xt_ready, 2 * (f["tile"] + TB))
                if opens(qb):
                    tokens(dict(tile=f["tile"] + TB), qb + 1)
                if qb == 0:
                    stack(f, qb, (0, 0))
                    load_wq(3, 0)
                    stack(f, qb, (0, 1))
                    maxima(f, qb, (0, 0))
                    stack(f, qb, (0, 2))

            def turn(f, qb, u, nf):
                r, k = u
                if nf is not None and k == NU - 2:
                    sp.wait_ge(q_ready, f["unit"] + NU)
                    sp.wait_ge(wq_loaded[2], f["wq"] + 16 * NP_)
                    for j in range(3):
                        load_wq(j, j)
                if reach(qb) > 2:
                    if units_left(u, 1):
                        maxima(f, qb, after(u, 1))
                    if units_left(u, 3):
                        sp.wait_ge(q_ready, unit0(f, u) + 2)
                        load_wq(min(k + 4, NU - 1), (k + 1) % NP_)
                        stack(f, qb, after(u, 3))
                elif units_left(u, 2):
                    sp.wait_ge(q_ready, unit0(f, u) + 1)
                    load_wq(5 + 2 * r if k == 2 else at(u) + 3, k)
                    stack(f, qb, after(u, 2))
                if units_left(u, 1):
                    if reach(qb) == 2:
                        maxima(f, qb, after(u, 1))
                elif nf is not None:
                    stack(nf, qb + 1, (0, 0))
                    stack(nf, qb + 1, (0, 1))

            with sp.Fori(0, NB) as b:
                for f, qb, nf in blocks(sp, b, prologue, turn):
                    if nf is not None:
                        maxima(nf, qb + 1, (0, 0))
                    for i in range(TB):
                        sp.wait_ge(x2_ready, f["tile"] + i + 1)
                        sp.dma_start(out_t[f["tile"] + i], xs[:, i, :]).then_inc(stored, 16)
                    sp.wait_ge(stored, 16 * (f["tile"] + TB))
                    if nf is None:
                        wait_apart(sp, wq_loaded[2], f["wq"] + 16 * NP_)

        @block.gpsimd
        def _(pool):
            c = [0]

            def step(ins):
                c[0] += 1
                ins.then_inc(pool_const, 1)
                pool.wait_ge(pool_const, c[0])

            step(nc.gpsimd.memset(ident[:, :], 0.0))
            step(nc.gpsimd.affine_select(out=ident[:, :], in_=ident[:, :], compare_op=ALU.not_equal, fill=1.0,
                                         base=0, pattern=[[-1, P]], channel_multiplier=1))
            step(nc.gpsimd.tensor_copy(identb[:, :], ident[:, :]))
            step(nc.gpsimd.memset(mask_qk[:, :], 0.0))
            step(nc.gpsimd.affine_select(out=mask_qk[:, :], in_=mask_qk[:, :], compare_op=ALU.is_ge, fill=NEG,
                                         base=0, pattern=[[-1, P]], channel_multiplier=1))
            step(nc.gpsimd.memset(mask_kq[:, :], 0.0))
            step(nc.gpsimd.affine_select(out=mask_kq[:, :], in_=mask_kq[:, :], compare_op=ALU.is_ge, fill=NEG,
                                         base=0, pattern=[[1, P]], channel_multiplier=-1))
            step(nc.gpsimd.memset(ones[:, :], 1.0))
            step(nc.gpsimd.memset(eps_sb[:, :], EPS))
            step(nc.gpsimd.memset(ks[STK:STK + 2, :].bitcast(F32), 1.0))
            for s, n in ((pv_done, CREDIT), (add_pool, CREDIT), (pv_sb, 1), (den_ready, 1)):
                for _ in range(n):
                    nc.gpsimd.memset(scratch[:, 0:1], 0.0).then_inc(s, 1)
                    pool.wait_ge(s, _ + 1)

            def prologue(f, qb):
                pass

            def add(f, qb, u, t):
                sums(pool, nc.gpsimd, add_pool, cp_pool, 0, pool_heads(qb, u), f, qb, u, t)

            def turn(f, qb, u, nf):
                for v, t in schedule(qb, u):
                    if t >= 2:
                        add(f, qb, v, t - 1)
                    elif t == 0:
                        add(f, qb, u, steps_of(qb) - 1)
                if not units_left(u, 1):
                    add(f, qb, u, steps_of(qb) - 1)

            with pool.Fori(0, NB) as b:
                for f, qb, nf in blocks(pool, b, prologue, turn):
                    wait_apart(pool, ao_ready, f["unit"] + NU)
                    for i in range(TB):
                        pool.wait_ge(z2_ready, f["tile"] + i + 1)
                        nc.gpsimd.tensor_tensor(xs[:, i, :], xs[:, i, :], zs[:, i, :], ALU.add).then_inc(x2_ready, 1)

        @block.scalar
        def _(act):
            act.wait_ge(pool_const, POOL_CONST)
            for n in range(CREDIT):
                nc.scalar.copy(scratch[:, 1:2], eps_sb[:, 0:1]).then_inc(exp_done, 1)
                act.wait_ge(exp_done, n + 1)
            def q_part(f, qb, u):
                act.wait_ge(q_ready, unit0(f, u) + 1)
                if not (isinstance(u[0], int) and u[1] == 0):
                    act.wait_ge(qs_loaded[(u[1] - 1) % NP_], filled(f, "stack", after(u, -1)))
                nc.scalar.copy(q1[:, :], ps[:, PQ, :]).then_inc(q1_sb, 1)

            def max_rows(f, qb, u, bank=None):
                bank = rows_bank(qb, u) if bank is None else bank
                act.wait_ge(mt_ready, unit0(f, u) + 1)
                if not (isinstance(u[0], int) and u[1] == 0):
                    act.wait_ge(qm_loaded[(u[1] - 1) % NP_], filled(f, "rows", after(u, -1)))
                nc.scalar.copy(mT[:, :], ps[0:2 * GH, bank, :]).then_inc(mt_sb, 1)

            def exps(f, qb, u, t, rows_of=None):
                T = steps_of(qb)
                s = step0(f, qb, u) + t
                c0, _ = cols(qb, t)
                slot = (u[1] * T + t) % NP_
                act.wait_ge(pv_done, CREDIT + s - NP_ + 1)
                a = adds0(f, qb, u) + (max(t - NP_, 1) if t >= NP_ else 1 - NP_ + t)
                act.wait_ge(add_pool, CREDIT + a)
                act.wait_ge(add_dve, CREDIT + a)
                for g in range(GH):
                    act.wait_ge(st_ready, head0(f, qb, u) + GH * t + g + 1)
                    bank = PST + g % 2
                    nc.scalar.activation(pr[:, slot, g, c0:], ps[:, bank, c0:], ACT.Exp, scale=SCALE).then_inc(exp_done, 1)
                    if g == 1 and rows_of is not None:
                        max_rows(f, qb, rows_of)

            def pv_copy(f, qb, u):
                act.wait_ge(pv_done, CREDIT + step0(f, qb, u) + steps_of(qb))
                nc.scalar.copy(ao[:, bass.ds(at(u), 1), :], ps[:, PPV:PPV + 1, :]).then_inc(pv_sb, 1)

            def piece(f, qb, what, i):
                if what == "tr":
                    act.wait_ge(xt_ready, 2 * (f["tile"] + i) + 1)
                    nc.scalar.copy(xT[:, 0:KT // 2, i * P:(i + 1) * P],
                                   ps[:, PM, :].rearrange("p (k c) -> p k c", c=P)).then_inc(xt_act, 1)
                elif what == "kv":
                    act.wait_ge(kv_ready, f["block"] + 1)
                    nc.scalar.copy(kv[3 * HD:4 * HD, :], ps[3 * HD:4 * HD, PQ, :]).then_inc(k_act, 1)
                    nc.scalar.copy(ks[2 * HD:3 * HD, qb * BLK:(qb + 1) * BLK], ps[2 * HD:3 * HD, PQ, :]).then_inc(k_act, 1)
                elif what == "q":
                    q_part(f, qb, (0, i))

            def prologue(f, qb):
                if qb == 0:
                    for i in range(TB):
                        piece(f, qb, "tr", i)
                    for what, i in (("kv", 0), ("q", 0), ("q", 1)):
                        piece(f, qb, what, i)
                    max_rows(f, qb, (0, 0))
                    piece(f, qb, "q", 2)
                    exps(f, qb, (0, 0), 0)
                for t in range(1, AHEAD):
                    exps(f, qb, (0, 0), t)

            def turn(f, qb, u, nf):
                T, lead = steps_of(qb), lead_of(qb)
                q_last = max(q_steps(qb))
                opened = opening(qb) if nf is not None and u[1] == NU - 1 else {}
                for v, t in schedule(qb, u):
                    exps(f, qb, v, t, after(u, 1) if v is u and t == T - lead and units_left(u, 1) else None)
                    for what, i in opened.get(t, []):
                        piece(nf, qb + 1, what, i)
                    if v is u and t == q_last and units_left(u, reach(qb)):
                        q_part(f, qb, after(u, reach(qb)))
                    if v is not u and t == 0:
                        pv_copy(f, qb, u)
                if not units_left(u, 1):
                    pv_copy(f, qb, u)
                for what, i in opened.get(END, []):
                    piece(nf, qb + 1, what, i)
                if opened:
                    piece(nf, qb + 1, "q", 1)

            def post(f, qb, nf):
                for stage, i in CLOSE_ACT:
                    n = f["tile"] + i
                    if stage == "proj":
                        act.wait_ge(y1_ready, n + 1)
                        nc.scalar.copy(zs[:, i, :], ps[:, PY:PY + 2, :].rearrange("p a c -> p (a c)")).then_inc(z1_ready, 1)
                    elif stage == "turn":
                        act.wait_ge(ht_ready, n + 1)
                        nc.scalar.copy(hT[:, i % 2, :, :],
                                       ps[:, pair(i):pair(i) + 2, :].rearrange("p a (k c) -> p (a k) c", c=P)).then_inc(ht_sb, 1)
                    elif stage == "low":
                        act.wait_ge(sm_ch, SM * n + 2)
                        nc.scalar.activation(le[:, i % 2, :], lg[:, i % 2, :], ACT.Exp, bias=nlm[:, i % 2, 0:1]).then_inc(le_ready, 1)
                    elif stage == "up":
                        act.wait_ge(slt_ready, n + 1)
                        nc.scalar.copy(slT[:, i % 2, :], ps[:, pair(i) + 1, 0:P]).then_inc(slt_sb, 1)
                    elif stage == "rows":
                        if nf is not None:
                            max_rows(nf, qb + 1, (0, 0), PY)
                    elif stage == "exps":
                        if nf is not None:
                            exps(nf, qb + 1, (0, 0), 0)
                    elif stage == "sum":
                        act.wait_ge(sh_ready, 2 * n + 2)
                        nc.scalar.activation(zs[:, i, :], ps[:, pair(i):pair(i) + 2, :].rearrange("p a c -> p (a c)"), ACT.Identity,
                                             scale=LN["ffn"]["r"][:, 0:1], bias=sh[:, i % 2, 1:2]).then_inc(z2_ready, 1)

            with act.Fori(0, NB) as b:
                for f, qb, nf in blocks(act, b, prologue, turn):
                    post(f, qb, nf)

        @block.vector
        def _(dve):
            dve.wait_ge(pool_const, POOL_CONST)
            c = [0]
            for s, n in ((add_dve, CREDIT), (mx_done, CREDIT), (rden_ready, 1)):
                for _ in range(n):
                    nc.vector.memset(scratch[:, 2:3], 0.0).then_inc(s, 1)
                    dve.wait_ge(s, _ + 1)
            for k in range(WT):
                dve.wait_ge(wt_ready, k + 1)
                bank = k % 4
                if k < KT:
                    nc.vector.tensor_copy(fa_sb[:, k, 0:HR], ps[:, bank, 0:P]).then_inc(wt_read, 1)
                elif k < 2 * KT:
                    nc.vector.tensor_copy(fa_sb[:, k - KT, HR:HR + NF], ps[:, bank, 0:NF]).then_inc(wt_read, 1)
                else:
                    n = k - 2 * KT
                    nc.vector.tensor_copy(fb_sb[:, n * P:(n + 1) * P], ps[:, bank, 0:P]).then_inc(wt_read, 1)

            def stats(kind, n, i, halves):
                L = LN[kind]
                for h, src in enumerate(halves):
                    nc.vector.bn_stats(L["st"][:, i, h, :], src).then_inc(L["s_st"], 1)
                wait_apart(dve, L["s_st"], 2 * (n + 1))
                nc.vector.bn_aggr(L["mv"][:, i, :], L["st"][:, i, :, :]).then_inc(L["s_mv"], 1)

            def rsqrt(kind, n, mv_count):
                L = LN[kind]
                s, at_ = L["s_ch"], [0]

                def chain(ins, wait=True):
                    ins.then_inc(s, 1)
                    at_[0] += 1
                    if wait:
                        dve.wait_ge(s, CH(kind) * n + at_[0])

                dve.wait_ge(L["s_mv"], mv_count)
                chain(nc.vector.tensor_scalar_add(L["ve"][:, :], L["mv"][:, :, 1], EPS))
                chain(nc.vector.tensor_single_scalar(L["half"][:, :], L["ve"][:, :].bitcast(I32), 1, op=ALU.logical_shift_right))
                if L["n"] == 1:
                    for k in range(1, ROUNDS):
                        chain(nc.vector.tensor_scalar_mul(L["c"][:, k, :], L["ve"][:, :], 0.25 ** k), wait=False)
                chain(nc.vector.tensor_scalar(L["y0"][:, :], L["half"][:, :], -1.0, float(MAGIC), ALU.mult, ALU.add))
                y = L["y0"][:, :].bitcast(F32)
                for k in range(ROUNDS):
                    if L["n"] == 1:
                        v = L["ve"][:, 0:1] if k == 0 else L["c"][:, k, 0:1]
                        chain(nc.vector.scalar_tensor_tensor(out=L["a"][:, k, :], in0=y, scalar=v, in1=y,
                                                             op0=ALU.mult, op1=ALU.mult))
                        vyy = L["a"][:, k, :]
                    else:
                        chain(nc.vector.scalar_tensor_tensor(out=L["a"][:, k, :], in0=y, scalar=0.25 ** k, in1=y,
                                                             op0=ALU.mult, op1=ALU.mult))
                        chain(nc.vector.tensor_tensor(L["c"][:, k, :], L["a"][:, k, :], L["ve"][:, :], ALU.mult))
                        vyy = L["c"][:, k, :]
                    chain(nc.vector.scalar_tensor_tensor(out=L["y"][:, k, :], in0=vyy, scalar=-3.0, in1=y,
                                                         op0=ALU.add, op1=ALU.mult))
                    y = L["y"][:, k, :]
                chain(nc.vector.tensor_scalar_mul(L["r"][:, :], y, (-0.5) ** ROUNDS))

            def q_rest(f, qb, u):
                dve.wait_ge(q1_sb, unit0(f, u) + 1)
                if not (isinstance(u[0], int) and u[1] == 0):
                    dve.wait_ge(qs_loaded[(u[1] - 1) % NP_], filled(f, "stack", after(u, -1)))
                nc.vector.tensor_tensor(q2[:, :], ps[:, PQ, :], q1[:, :].bitcast(F32), ALU.subtract).then_inc(q2_sb, 1)

            def maxima(f, qb, u, s):
                c_, qt, n, _ = item(qb, s)
                for g in range(GH):
                    dve.wait_ge(mx_ready, head0(f, qb, u) + GH * s + g + 1)
                    nc.vector.tensor_reduce(mx[:, qt * GH + g, c_:c_ + 1], ps[:, mx_bank(qb, u, s, g), 0:n], AX.X,
                                            ALU.max).then_inc(mx_done, 1)
                if s == steps_of(qb) - 1:
                    j = unit0(f, u) + 1
                    dve.wait_ge(mx_done, CREDIT + head0(f, qb, u) + GH * (s + 1))
                    nc.vector.tensor_reduce(negm[:, :], mx[:, :, 0:qb + 1], AX.X, ALU.max, negate=True).then_inc(negm_ready, 1)
                    dve.wait_ge(negm_ready, j)
                    m_v = negm[:, :].rearrange("p (t g) -> p t g", g=GH)
                    nc.vector.tensor_copy(mz[:, :, :, 0].bitcast(F32R), m_v).then_inc(mz1_ready, 1)
                    dve.wait_ge(mz1_ready, j)
                    nc.vector.tensor_tensor(mz[:, :, :, 1].bitcast(F32R), m_v, mz[:, :, :, 0], ALU.subtract).then_inc(mz_ready, 1)

            def add(f, qb, u, t):
                sums(dve, nc.vector, add_dve, cp_dve, pool_heads(qb, u), GH, f, qb, u, t)

            def divide(f, qb, u):
                n = unit0(f, u) + 1
                dve.wait_ge(den_ready, 1 + n)
                nc.vector.reciprocal(rden[:, :], ps[:, PAUX, :]).then_inc(rden_ready, 1)
                dve.wait_ge(rden_ready, 1 + n)
                dve.wait_ge(pv_sb, 1 + n)
                a = ao[:, bass.ds(at(u), 1), :]
                nc.vector.tensor_tensor(a, a, rden[:, None, :], ALU.mult).then_inc(ao_ready, 1)

            def bring(f, parts):
                base = f["tile"]
                for part in parts:
                    if part < TB:
                        dve.wait_ge(x_loaded[part], 16 * (f["block"] + 1))
                        stats("pre", base + part, part, [t4[:, part, h * HALF:(h + 1) * HALF] for h in range(2)])
                    elif part == TB:
                        rsqrt("pre", f["block"], base + TB)
                    else:
                        i = part - TB - 1
                        nc.vector.tensor_scalar(t4[:, i, :], t4[:, i, :], LN["pre"]["mv"][:, i, 0:1], LN["pre"]["r"][:, i:i + 1],
                                                ALU.subtract, ALU.mult).then_inc(xn_ready, 1)

            def piece(f, qb, what, i):
                n = f["block"]
                if what == "tr":
                    dve.wait_ge(xt_ready, 2 * (f["tile"] + i) + 2)
                    nc.vector.tensor_copy(xT[:, KT // 2:KT, i * P:(i + 1) * P],
                                          ps[:, PM + 1, :].rearrange("p (k c) -> p k c", c=P)).then_inc(xt_dve, 1)
                elif what == "kv":
                    here = slice(qb * BLK, (qb + 1) * BLK)
                    dve.wait_ge(kv_ready, n + 1)
                    nc.vector.tensor_copy(kv[HD:2 * HD, :].bitcast(F32R), ps[HD:2 * HD, PQ, :]).then_inc(k_dve, 1)
                    nc.vector.tensor_copy(ks[0:HD, here], ps[0:HD, PQ, :]).then_inc(k_dve, 1)
                    dve.wait_ge(k_dve, 3 * n + 1)
                    nc.vector.tensor_tensor(ks[HD:2 * HD, here], ps[HD:2 * HD, PQ, :], kv[HD:2 * HD, :],
                                            ALU.subtract).then_inc(k_dve, 1)
                elif what == "vt":
                    dve.wait_ge(v_tr, n + 1)
                    nc.vector.tensor_copy(vs[:, TB * qb:TB * (qb + 1), :],
                                          ps[:, PAUX, 0:TB * HD].rearrange("p (t d) -> p t d", d=HD)).then_inc(v_sb, 1)
                else:
                    q_rest(f, qb, (0, i))

            def prologue(f, qb):
                if qb == 0:
                    bring(f, range(2 * TB + 1))
                    for i in range(TB):
                        piece(f, qb, "tr", i)
                    for what, i in (("kv", 0), ("vt", 0), ("q", 0), ("q", 1)):
                        piece(f, qb, what, i)
                    for u, s in early_items(qb):
                        maxima(f, qb, u, s)
                    piece(f, qb, "q", 2)
                for t in range(AHEAD):
                    maxima(f, qb, *normal(qb, (0, 1), t + lead_of(qb)))

            def turn(f, qb, u, nf):
                T, lead = steps_of(qb), lead_of(qb)
                q_last = max(q_steps(qb))
                opened = opening(qb) if nf is not None and u[1] == NU - 1 else {}
                bringing = nf is not None and u[1] == NU - 2
                for j, (v, t) in enumerate(schedule(qb, u)):
                    w, s = normal(qb, after(v, 1), t + lead)
                    if not isinstance(w[0], int) or w[1] < NU:
                        maxima(f, qb, w, s)
                    for what, i in opened.get(t, []):
                        piece(nf, qb + 1, what, i)
                    if bringing:
                        n = 2 * TB + 1
                        bring(nf, range(n * j // T, n * (j + 1) // T))
                    if t >= 2:
                        add(f, qb, v, t - 1)
                    elif t == 0:
                        add(f, qb, u, T - 1)
                    if reach(qb) > 2 and v is u and t == T - 1 and u[1] > 0:
                        divide(f, qb, after(u, -1))
                    if v is u and t == q_last and units_left(u, reach(qb)):
                        q_rest(f, qb, after(u, reach(qb)))
                if not units_left(u, 1):
                    add(f, qb, u, T - 1)
                for what, i in opened.get(END, []):
                    piece(nf, qb + 1, what, i)
                if reach(qb) == 2 or not units_left(u, 1):
                    divide(f, qb, u)
                if opened:
                    piece(nf, qb + 1, "q", 1)

            def post(f, qb, nf):
                base = f["tile"]
                for stage, i in CLOSE_DVE:
                    n = base + i
                    if stage == "max":
                        for u, s in portion(qb, i):
                            maxima(nf, qb + 1, u, s)
                    elif stage == "proj":
                        dve.wait_ge(z1_ready, n + 1)
                        stats("att", n, 0, [zs[:, i, h * HALF:(h + 1) * HALF] for h in range(2)])
                        rsqrt("att", n, n + 1)
                        dve.wait_ge(r_loaded[i], 16 * (f["block"] + 1))
                        nc.vector.scalar_tensor_tensor(out=xs[:, i, :], in0=zs[:, i, :], scalar=LN["att"]["r"][:, 0:1],
                                                       in1=xs[:, i, :], op0=ALU.mult, op1=ALU.add).then_inc(x1_ready, 1)
                        nc.vector.tensor_tensor(m1[:, i:i + 1], LN["att"]["mv"][:, 0, 0:1], LN["att"]["r"][:, 0:1],
                                                ALU.mult).then_inc(m1_ready, 1)
                        dve.wait_ge(x1_ready, n + 1)
                        stats("mid", n, 0, [xs[:, i, h * HALF:(h + 1) * HALF] for h in range(2)])
                        rsqrt("mid", n, n + 1)
                        nc.vector.tensor_scalar(xn[:, i, :], xs[:, i, :], LN["mid"]["mv"][:, 0, 0:1], LN["mid"]["r"][:, 0:1],
                                                ALU.subtract, ALU.mult).then_inc(h_ready, 1)
                    elif stage == "low":
                        dve.wait_ge(low_ready, n + 1)
                        k = i % 2
                        m = SM * n
                        low = ps[:, pair(i), :]
                        nc.vector.tensor_tensor(lg[:, k, :], low[:, HR:HR + NF], br_sb[:, :], ALU.add).then_inc(sm_ch, 1)
                        dve.wait_ge(sm_ch, m + 1)
                        nc.vector.tensor_reduce(nlm[:, k, :], lg[:, k, :], AX.X, ALU.max, negate=True).then_inc(sm_ch, 1)
                        dve.wait_ge(le_ready, n + 1)
                        nc.vector.tensor_reduce(ls[:, k, :], le[:, k, :], AX.X, ALU.add).then_inc(sm_ch, 1)
                        dve.wait_ge(sm_ch, m + 3)
                        nc.vector.reciprocal(lr[:, k, :], ls[:, k, :]).then_inc(sm_ch, 1)
                        dve.wait_ge(sm_ch, m + 4)
                        nc.vector.tensor_scalar(lw[:, k, :], le[:, k, :], lr[:, k, 0:1], NF * SCALING, ALU.mult, ALU.mult).then_inc(sm_ch, 1)
                        dve.wait_ge(sm_ch, m + 5)
                        nc.vector.tensor_tensor(sl[:, k, :].rearrange("p (h r) -> p h r", h=NF),
                                                low[:, 0:HR].rearrange("p (h r) -> p h r", h=NF),
                                                lw[:, k, :, None].to_broadcast([P, NF, RANK]), ALU.mult).then_inc(sl_ready, 1)
                    else:
                        if i >= 1:
                            dve.wait_ge(z2_ready, n)
                        dve.wait_ge(y2_ready, n + 1)
                        stats("ffn", n, 0, [ps[:, pair(i) + h, :] for h in range(2)])
                        rsqrt("ffn", n, n + 1)
                        dve.wait_ge(m1_ready, n + 1)
                        nc.vector.tensor_tensor(sh[:, i % 2, 0:1], LN["ffn"]["mv"][:, 0, 0:1], LN["ffn"]["r"][:, 0:1],
                                                ALU.mult).then_inc(sh_ready, 1)
                        dve.wait_ge(sh_ready, 2 * n + 1)
                        nc.vector.scalar_tensor_tensor(out=sh[:, i % 2, 1:2], in0=sh[:, i % 2, 0:1], scalar=-1.0, in1=m1[:, i:i + 1],
                                                       op0=ALU.mult, op1=ALU.subtract).then_inc(sh_ready, 1)
                dve.wait_ge(z2_ready, base + TB)

            with dve.Fori(0, NB) as b:
                for f, qb, nf in blocks(dve, b, prologue, turn):
                    post(f, qb, nf)

        @block.tensor
        def _(pe):
            pe.wait_ge(pool_const, POOL_CONST)
            pe.wait_ge(const_loaded, 16 * N_CONST)
            for k in range(WT):
                bank = k % 4
                if k >= 4:
                    pe.wait_ge(wt_read, k - 3)
                if k < KT:
                    nc.tensor.transpose(ps[:, bank, 0:P], xs[:, 0, k * P:(k + 1) * P], ident[:, :]).then_inc(wt_ready, 1)
                elif k < 2 * KT:
                    n = k - KT
                    nc.tensor.transpose(ps[:, bank, 0:NF], xs[0:NF, 1, n * P:(n + 1) * P], ident[0:NF, 0:NF]).then_inc(wt_ready, 1)
                else:
                    n = k - 2 * KT
                    nc.tensor.transpose(ps[:, bank, 0:P], xs[:, 2, n * P:(n + 1) * P], ident[:, :]).then_inc(wt_ready, 1)
            pe.wait_ge(wt_read, WT)

            def project(f, qb, u, tiles):
                if 0 in tiles:
                    pe.wait_ge(wq_loaded[u[1] % NP_], f["wq"] + 16 * (u[1] // NP_ + 1))
                    if not (isinstance(u[0], int) and u[1] == 0):
                        pe.wait_ge(q1_sb, unit0(f, u))
                        pe.wait_ge(q2_sb, unit0(f, u))
                        if reach(qb) > 2 and u[1] >= reach(qb):
                            pe.wait_ge(mt_sb, unit0(f, u) - 1)
                for k in tiles:
                    last = nc.tensor.matmul(ps[:, PQ, :], wq_sb[:, u[1] % NP_, k, :], xT[:, k, :],
                                            start=(k == 0), stop=(k == KT - 1))
                if KT - 1 in tiles:
                    last.then_inc(q_ready, 1)

            def max_scores(f, qb, u, s, g):
                c, qt, n, diagonal = item(qb, s)
                if s == 0 and g == 0:
                    pe.wait_ge(qs_loaded[u[1] % NP_], filled(f, "stack", u))
                n_ = GH * s + g
                behind = 1 if is_early(qb, u, s) else n_ - GH * lead_of(qb) if first_of_three(qb, u, s, g) else 2
                pe.wait_ge(mx_done, CREDIT + head0(f, qb, u) + n_ - behind)
                bank = mx_bank(qb, u, s, g)
                last = nc.tensor.matmul(ps[:, bank, 0:n], qs[0:STK, u[1] % NP_, g, qt * P:(qt + 1) * P],
                                        ks[0:STK, c * BLK:c * BLK + n], start=True, stop=not diagonal)
                if diagonal:
                    last = nc.tensor.matmul(ps[:, bank, n - P:n], identb[:, :], mask_qk[:, :], start=False, stop=True)
                last.then_inc(mx_ready, 1)

            def scores(f, qb, u, t, g):
                T = steps_of(qb)
                c0, diagonal = cols(qb, t)
                if t == 0 and g == 0:
                    pe.wait_ge(qm_loaded[u[1] % NP_], filled(f, "rows", u))
                n = head0(f, qb, u) + GH * t + g
                bank = PST + g % 2
                pe.wait_ge(exp_done, CREDIT + n - 2 + 1)
                last = nc.tensor.matmul(ps[:, bank, c0:], ks[0:STK + 2, t * P:(t + 1) * P],
                                        qs[0:STK + 2, u[1] % NP_, g, c0:], start=True, stop=not diagonal)
                if diagonal:
                    last = nc.tensor.matmul(ps[:, bank, c0:c0 + P], identb[:, :], mask_kq[:, :], start=False, stop=True)
                last.then_inc(st_ready, 1)

            def values(f, qb, u, t):
                T = steps_of(qb)
                c0, _ = cols(qb, t)
                if t == 0:
                    pe.wait_ge(pv_sb, 1 + unit0(f, u))
                for g in range(GH):
                    pe.wait_ge(exp_done, CREDIT + head0(f, qb, u) + GH * t + g + 1)
                    last = nc.tensor.matmul(ps[g * HD:(g + 1) * HD, PPV, c0:], vs[:, t, :], pr[:, (u[1] * T + t) % NP_, g, c0:],
                                            start=(t == 0), stop=(t == T - 1))
                last.then_inc(pv_done, 1)

            def max_transposes(f, qb, u, bank=None):
                bank = rows_bank(qb, u) if bank is None else bank
                pe.wait_ge(mz_ready, unit0(f, u) + 1)
                if bank == PQ:
                    n = unit0(f, u) + (2 if u[1] + 1 < NU else 1)
                    pe.wait_ge(q1_sb, n)
                    pe.wait_ge(q2_sb, n)
                elif not (isinstance(u[0], int) and u[1] == 0):
                    pe.wait_ge(rden_ready, 1 + unit0(f, u) - 1)
                for qt in range(TB):
                    last = nc.tensor.transpose(ps[0:2 * GH, bank, qt * P:(qt + 1) * P],
                                               mz[:, qt, :, :].rearrange("p g c -> p (g c)"), ident[:, :])
                last.then_inc(mt_ready, 1)

            def sum_keys(f, qb, u):
                n = adds0(f, qb, u) + steps_of(qb) - 1
                pe.wait_ge(add_pool, CREDIT + n)
                pe.wait_ge(add_dve, CREDIT + n)
                if rows_bank(qb, after(u, 1)) == PAUX and units_left(u, 1):
                    pe.wait_ge(mt_sb, unit0(f, u) + 2)
                elif rows_bank(qb, after(u, 1)) != PAUX and u[1] > 0:
                    pe.wait_ge(rden_ready, 1 + unit0(f, u))
                for g in range(GH):
                    last = nc.tensor.matmul(ps[g * HD:(g + 1) * HD, PAUX, :], ones[:, :], ds[:, g, :], start=True, stop=True)
                last.then_inc(den_ready, 1)

            def step(f, qb, u, t, prev, rows_of=None):
                w, s = normal(qb, after(u, 1), t + lead_of(qb))
                more = not isinstance(w[0], int) or w[1] < NU
                for g in range(GH):
                    scores(f, qb, u, t, g)
                    if more:
                        max_scores(f, qb, w, s, g)
                    if g == 1 and rows_of is not None:
                        max_transposes(f, qb, rows_of)
                if t >= 1:
                    values(f, qb, u, t - 1)
                elif prev is not None:
                    values(f, qb, prev, steps_of(qb) - 1)

            def piece(f, qb, what, i):
                base, n = f["tile"], f["block"] + 1
                if what == "tr":
                    pe.wait_ge(xn_ready, base + i + 1)
                    for h in range(2):
                        if i >= 1:
                            pe.wait_ge((xt_act, xt_dve)[h], base + i)
                        for k in range(KT // 2):
                            kk = h * KT // 2 + k
                            last = nc.tensor.transpose(ps[:, PM + h, k * P:(k + 1) * P], t4[:, i, kk * P:(kk + 1) * P], ident[:, :])
                        last.then_inc(xt_ready, 1)
                elif what == "kv":
                    pe.wait_ge(xt_act, base + TB)
                    pe.wait_ge(xt_dve, base + TB)
                    for k in range(KT):
                        last = nc.tensor.matmul(ps[:, PQ, :], wkv_sb[:, k, :], xT[:, k, :], start=(k == 0), stop=(k == KT - 1))
                    last.then_inc(kv_ready, 1)
                elif what == "vt":
                    if qb > 0:
                        pe.wait_ge(rden_ready, 1 + f["unit"] - 1)
                    wait_apart(pe, k_act, 2 * n)
                    for k in range(TB):
                        last = nc.tensor.transpose(ps[:, PAUX, k * HD:(k + 1) * HD], kv[3 * HD:4 * HD, k * P:(k + 1) * P],
                                                   ident[3 * HD:4 * HD, 3 * HD:4 * HD])
                    last.then_inc(v_tr, 1)
                else:
                    if i == 0:
                        pe.wait_ge(k_dve, 3 * n)
                    project(f, qb, (0, i), range(KT))

            def early(f, qb, items):
                for u, s in items:
                    for g in range(GH):
                        max_scores(f, qb, u, s, g)

            def prologue(f, qb):
                if qb == 0:
                    for i in range(TB):
                        piece(f, qb, "tr", i)
                    for what, i in (("kv", 0), ("vt", 0), ("q", 0), ("q", 1)):
                        piece(f, qb, what, i)
                    early(f, qb, early_items(qb))
                    pe.wait_ge(v_sb, f["block"] + 1)
                    max_transposes(f, qb, (0, 0))
                    piece(f, qb, "q", 2)
                for t in range(AHEAD):
                    step(f, qb, (0, 0), t, None)
                if qb > 0:
                    wait_apart(pe, z2_ready, f["tile"])

            def turn(f, qb, u, nf):
                T, lead = steps_of(qb), lead_of(qb)
                q_at = q_steps(qb)
                opened = opening(qb) if nf is not None and u[1] == NU - 1 else {}
                for v, t in schedule(qb, u):
                    if reach(qb) == 2 and v is u and t in q_at and units_left(u, 2):
                        project(f, qb, after(u, 2), q_at[t])
                    step(f, qb, v, t, u, after(u, 1) if v is u and t == T - lead and units_left(u, 1) else None)
                    for what, i in opened.get(t, []):
                        piece(nf, qb + 1, what, i)
                    if reach(qb) > 2 and v is u and t in q_at and units_left(u, reach(qb)):
                        project(f, qb, after(u, reach(qb)), q_at[t])
                if not units_left(u, 1):
                    values(f, qb, u, T - 1)
                for what, i in opened.get(END, []):
                    piece(nf, qb + 1, what, i)
                if opened:
                    pe.wait_ge(v_sb, nf["block"] + 1)
                sum_keys(f, qb, u)
                if opened:
                    piece(nf, qb + 1, "q", 1)

            def post(f, qb, nf):
                base = f["tile"]
                pe.wait_ge(ao_ready, f["unit"] + NU)
                for stage, i in CLOSE_PE:
                    part = i % 4
                    if stage == "proj":
                        i = i // 4
                    n = base + i
                    if stage == "max":
                        early(nf, qb + 1, portion(qb, i))
                    elif stage == "proj":
                        if i >= 1 and part == 0:
                            pe.wait_ge(z1_ready, n)
                        h = part // 2
                        for k in range(part % 2 * KT // 2, (part % 2 + 1) * KT // 2):
                            last = nc.tensor.matmul(ps[:, PY + h, :], ao[:, k, i * P:(i + 1) * P],
                                                    wo_sb[:, k, h * HALF:(h + 1) * HALF], start=(k == 0), stop=(k == KT - 1))
                        if part == 3:
                            last.then_inc(y1_ready, 1)
                    elif stage == "turn":
                        pe.wait_ge(h_ready, n + 1)
                        if i >= 2:
                            pe.wait_ge(z2_ready, n - 1)
                        elif i == 1 and nf is not None:
                            pe.wait_ge(q2_sb, nf["unit"] + 2)
                        for h in range(2):
                            for k in range(KT // 2):
                                kk = h * KT // 2 + k
                                last = nc.tensor.transpose(ps[:, pair(i) + h, k * P:(k + 1) * P], xn[:, i, kk * P:(kk + 1) * P], ident[:, :])
                        last.then_inc(ht_ready, 1)
                    elif stage == "rows":
                        if nf is not None:
                            pe.wait_ge(z1_ready, base + TB)
                            max_transposes(nf, qb + 1, (0, 0), PY)
                    elif stage == "low":
                        pe.wait_ge(ht_sb, n + 1)
                        for k in range(KT):
                            last = nc.tensor.matmul(ps[:, pair(i), 0:HR + NF], hT[:, i % 2, k, :], fa_sb[:, k, :],
                                                    start=(k == 0), stop=(k == KT - 1))
                        last.then_inc(low_ready, 1)
                    else:
                        pe.wait_ge(sl_ready, n + 1)
                        nc.tensor.transpose(ps[:, pair(i) + 1, 0:P], sl[:, i % 2, :], ident[:, :]).then_inc(slt_ready, 1)
                        pe.wait_ge(slt_sb, n + 1)
                        for h in range(2):
                            last = nc.tensor.matmul(ps[:, pair(i) + h, :], slT[:, i % 2, :], fb_sb[:, h * HALF:(h + 1) * HALF],
                                                    start=True, stop=True)
                        last.then_inc(y2_ready, 1)
                pe.wait_ge(z2_ready, base + (TB if nf is None else TB - 1))

            with pe.Fori(0, NB) as b:
                for f, qb, nf in blocks(pe, b, prologue, turn):
                    post(f, qb, nf)


_INS = ['L0_attn_x', 'L0_attn_wq', 'L0_attn_wk', 'L0_attn_wv', 'L0_attn_wo', 'L0_ffn_A', 'L0_ffn_B', 'L0_ffn_Wr', 'L0_ffn_br']


def kernel(**inputs):
    import numpy as _np
    import concourse.bacc as _bacc
    from concourse import mybir as _mybir
    from concourse.bass_utils import run_bass_kernel_spmd as _run

    nc = _bacc.Bacc("TRN2", target_bir_lowering=False, num_devices=1)
    arrays, args = {}, []
    for name in _INS:
        a = _np.ascontiguousarray(inputs[name])
        arrays[f"in_{name}_dram"] = a
        args.append(nc.dram_tensor(f"in_{name}_dram", a.shape, _mybir.dt.from_np(a.dtype), kind="ExternalInput").ap())
    shape = tuple(inputs["L0_attn_x"].shape)
    args.append(nc.dram_tensor("out_0_dram", shape, _mybir.dt.from_np(_np.dtype("float32")), kind="ExternalOutput").ap())
    bass_mqa_sandwich_lora_router(nc, *args)
    r = _run(nc, [arrays], core_ids=[0])
    return r.results[0]["out_0_dram"]
```
